# Optimizing a Trainium2 kernel written in Bass

```python
import numpy as np
import jax
import jax.numpy as jnp

def _softmax(x, axis=-1):
    return jax.nn.softmax(x, axis=axis)

def _gelu(x):
    return jax.nn.gelu(x, approximate=True)

def _silu(x):
    return jax.nn.silu(x)

def _sigmoid(x):
    return jax.nn.sigmoid(x)

def _layernorm(x, axis=-1, eps=1e-05):
    m = jnp.mean(x, axis=axis, keepdims=True)
    v = jnp.var(x, axis=axis, keepdims=True)
    return (x - m) / jnp.sqrt(v + eps)

def _scatter_add(tgt, idx, src, axis=0):
    return tgt.at[idx].add(src)

def _segment_sum(src, seg, n):
    return jax.ops.segment_sum(src, seg, n)
kernel_name = 'mk_gnn_preln_d4_gnn_r32_029a3e'

def setup_inputs(seed: int=0):
    np.random.seed(seed)
    _w = jnp.asarray

    def _rec_inputs():
        import jax
        import jax.numpy as jnp
        _gk = jax.random.key(seed)
        x = -0.000202 + 1 * jax.random.normal(jax.random.fold_in(_gk, 1), (3125, 64), jnp.float32)
        _s = jax.random.randint(jax.random.fold_in(_gk, 2), (50000,), 0, 3125, jnp.int32)
        _d = jax.random.randint(jax.random.fold_in(_gk, 3), (50000,), 0, 3125, jnp.int32)
        _loop = jnp.arange(3125, dtype=jnp.int32)
        src = jnp.concatenate([_s, _d, _loop])
        dst = jnp.concatenate([_d, _s, _loop])
        _o = jnp.argsort(dst, stable=True)
        src = src[_o]
        dst = dst[_o]
        edge_attr_16 = -4.12889e-05 + 1 * jax.random.normal(jax.random.fold_in(_gk, 12), (103125, 16), jnp.float32)
        edge_type_16 = jax.random.randint(jax.random.fold_in(_gk, 14), (103125,), 0, 16, jnp.int32)
        edge_weight1 = jax.random.uniform(jax.random.fold_in(_gk, 15), (103125, 1), jnp.float32, 0.0, 1)
        return (x, src, dst, edge_attr_16, edge_type_16, edge_weight1)
    x, src, dst, edge_attr_16, edge_type_16, edge_weight1 = _rec_inputs()

    def _L0_gnn_setup():
        import jax, jax.numpy as jnp
        import numpy as np
        N_NODES = 3125
        key = jax.random.key(seed)
        k1, k2 = jax.random.split(key)
        x = jax.random.normal(k1, (N_NODES, 64), dtype=jnp.float32)
        edge_index = jax.random.randint(k2, (2, 50000), 0, N_NODES, dtype=jnp.int64)
        return {'x': x, 'edge_index': edge_index}
    _L0_gnn_all = _L0_gnn_setup()
    _L0_gnn_in = {k: v for k, v in _L0_gnn_all.items() if k in ()}
    del _L0_gnn_all

    def _L1_gnn_setup():
        import jax, jax.numpy as jnp
        import numpy as np
        N_NODES = 3125
        N_EDGES = 100000
        IN_FEAT = 64
        OUT_FEAT = 64
        NUM_RELS = 16
        key = jax.random.key(seed)
        k1, k2, k3, k4, k5, k6 = jax.random.split(key, 6)
        h = jax.random.normal(k1, (N_NODES, IN_FEAT), dtype=jnp.float32)
        weight = jax.random.normal(k2, (NUM_RELS, IN_FEAT, OUT_FEAT), dtype=jnp.float32) * 0.1
        norm = jax.random.uniform(k3, (N_EDGES, 1), dtype=jnp.float32)
        src = jax.random.randint(k4, (N_EDGES,), 0, N_NODES, dtype=jnp.int32)
        dst = jax.random.randint(k5, (N_EDGES,), 0, N_NODES, dtype=jnp.int32)
        rel_type = jax.random.randint(k6, (N_EDGES,), 0, NUM_RELS, dtype=jnp.int32)
        return {'h': h, 'weight': weight, 'norm': norm, 'src': src, 'dst': dst, 'rel_type': rel_type}
    _L1_gnn_all = _L1_gnn_setup()
    _L1_gnn_in = {k: v for k, v in _L1_gnn_all.items() if k in ('weight',)}
    del _L1_gnn_all

    def _L2_gnn_setup():
        import jax, jax.numpy as jnp
        import numpy as np
        N, E, D = (3125, 50000, 64)
        K = 3
        LAMBDA_AMP = 0.1
        key = jax.random.key(seed)
        k1, k2 = jax.random.split(key)
        x = jax.random.normal(k1, (N, D), dtype=jnp.float32)
        edge_index = jax.random.randint(k2, (2, E), 0, N, dtype=jnp.int32)
        return {'x': x, 'edge_index': edge_index}
    _L2_gnn_all = _L2_gnn_setup()
    _L2_gnn_in = {k: v for k, v in _L2_gnn_all.items() if k in ()}
    del _L2_gnn_all

    def _L3_gnn_setup():
        import jax, jax.numpy as jnp
        import numpy as np
        N_NODES = 50000
        N_EDGES = 12500
        EMB = 64
        EDGE_F = 16
        HEADS = 2
        N_LAYERS = 5
        NEG_SLOPE = 0.2

        def _gat_layer(x, src_f, dst_f, edge_attr_full, W, b, eW, eb, att):
            N = x.shape[0]
            C = EMB
            edge_emb = (edge_attr_full @ eW.T + eb).reshape(-1, HEADS, C)
            xt = x @ W
            x_j = xt[src_f].reshape(-1, HEADS, C) + edge_emb
            x_i = xt[dst_f].reshape(-1, HEADS, C)
            alpha = (jnp.concatenate([x_i, x_j], axis=-1) * att[None]).sum(-1)
            alpha = jax.nn.leaky_relu(alpha, NEG_SLOPE)
            amax = jax.ops.segment_max(alpha, dst_f, num_segments=N)[dst_f]
            ex = jnp.exp(alpha - amax)
            denom = jax.ops.segment_sum(ex, dst_f, num_segments=N)[dst_f] + 1e-16
            a = ex / denom
            out = jax.ops.segment_sum(x_j * a[..., None], dst_f, num_segments=N)
            return out.mean(axis=1) + b
        key = jax.random.key(seed)
        ks = jax.random.split(key, 10)
        x = jax.random.normal(ks[0], (N_NODES, EMB), dtype=jnp.float32)
        src = jax.random.randint(ks[1], (N_EDGES,), 0, N_NODES, dtype=jnp.int32)
        off = jax.random.randint(ks[2], (N_EDGES,), 1, N_NODES, dtype=jnp.int32)
        dst = (src + off) % N_NODES
        edge_index = jnp.stack([src, dst], axis=0)
        edge_attr = jax.random.normal(ks[3], (N_EDGES, EDGE_F), dtype=jnp.float32)
        g = 0.1
        weights = jax.random.normal(ks[4], (N_LAYERS, EMB, HEADS * EMB), dtype=jnp.float32) * g
        biases = jnp.zeros((N_LAYERS, EMB), dtype=jnp.float32)
        edge_ws = jax.random.normal(ks[5], (N_LAYERS, HEADS * EMB, EDGE_F), dtype=jnp.float32) * g
        edge_bs = jnp.zeros((N_LAYERS, HEADS * EMB), dtype=jnp.float32)
        atts = jax.random.normal(ks[6], (N_LAYERS, HEADS, 2 * EMB), dtype=jnp.float32) * g
        return {'x': x, 'edge_index': edge_index, 'edge_attr': edge_attr, 'weights': weights, 'biases': biases, 'edge_ws': edge_ws, 'edge_bs': edge_bs, 'atts': atts}
    _L3_gnn_all = _L3_gnn_setup()
    _L3_gnn_in = {k: v for k, v in _L3_gnn_all.items() if k in ('weights', 'biases', 'edge_ws', 'edge_bs', 'atts')}
    del _L3_gnn_all
    return {'x': x, 'src': src, 'dst': dst, 'edge_attr_16': edge_attr_16, 'edge_type_16': edge_type_16, 'edge_weight1': edge_weight1, 'L1_gnn_weight': _L1_gnn_in['weight'], 'L3_gnn_weights': _L3_gnn_in['weights'], 'L3_gnn_biases': _L3_gnn_in['biases'], 'L3_gnn_edge_ws': _L3_gnn_in['edge_ws'], 'L3_gnn_edge_bs': _L3_gnn_in['edge_bs'], 'L3_gnn_atts': _L3_gnn_in['atts']}

def reference(x, src, dst, edge_attr_16, edge_type_16, edge_weight1, L1_gnn_weight, L3_gnn_weights, L3_gnn_biases, L3_gnn_edge_ws, L3_gnn_edge_bs, L3_gnn_atts):
    import jax
    import jax.numpy as jnp

    def _L0_gnn_ref(x, edge_index):
        import jax, jax.numpy as jnp
        import numpy as np
        N_NODES = 3125
        src, dst = (edge_index[0], edge_index[1])
        msgs = x[src]
        out = jax.ops.segment_sum(msgs, dst, num_segments=x.shape[0])
        return out

    def _L1_gnn_ref(h, weight, norm, src, dst, rel_type):
        import jax, jax.numpy as jnp
        import numpy as np
        N_NODES = 3125
        N_EDGES = 100000
        IN_FEAT = 64
        OUT_FEAT = 64
        NUM_RELS = 16
        n_nodes = h.shape[0]
        transformed = jnp.einsum('nd,rdo->nro', h, weight)
        msg = transformed[src, rel_type] * norm
        agg = jax.ops.segment_sum(msg, dst, num_segments=n_nodes)
        return jax.nn.relu(agg)

    def _L2_gnn_ref(x, edge_index):
        import jax, jax.numpy as jnp
        import numpy as np
        N, E, D = (3125, 50000, 64)
        K = 3
        LAMBDA_AMP = 0.1
        n = x.shape[0]
        row, col = (edge_index[0], edge_index[1])
        loop = jnp.arange(n, dtype=edge_index.dtype)
        row = jnp.concatenate([row, loop])
        col = jnp.concatenate([col, loop])
        w = jnp.ones(row.shape[0], dtype=x.dtype)
        deg = jax.ops.segment_sum(w, col, num_segments=n)
        dinv = jnp.where(deg > 0, jax.lax.rsqrt(deg), jnp.zeros_like(deg))
        w = dinv[row] * w * dinv[col]
        gamma = 1.0 / (2.0 * (1.0 - LAMBDA_AMP))
        lam = gamma * LAMBDA_AMP

        def spmm(z):
            return jax.ops.segment_sum(z[col] * w[:, None], row, num_segments=n)
        hh = x
        for _ in range(K):
            y = x - gamma * 2.0 * (1.0 - LAMBDA_AMP) * (x - spmm(x))
            d = y - hh
            rn = jnp.sqrt(jnp.sum(d * d, axis=1))
            score = jnp.where(rn > 0, jnp.maximum(rn - lam, 0.0) / jnp.where(rn > 0, rn, 1.0), 0.0)
            x = hh + score[:, None] * d
        return x

    def _L3_gnn_ref(x, edge_index, edge_attr, weights, biases, edge_ws, edge_bs, atts):
        import jax, jax.numpy as jnp
        import numpy as np
        N_NODES = 50000
        N_EDGES = 12500
        EMB = 64
        EDGE_F = 16
        HEADS = 2
        N_LAYERS = 5
        NEG_SLOPE = 0.2

        def _gat_layer(x, src_f, dst_f, edge_attr_full, W, b, eW, eb, att):
            N = x.shape[0]
            C = EMB
            edge_emb = (edge_attr_full @ eW.T + eb).reshape(-1, HEADS, C)
            xt = x @ W
            x_j = xt[src_f].reshape(-1, HEADS, C) + edge_emb
            x_i = xt[dst_f].reshape(-1, HEADS, C)
            alpha = (jnp.concatenate([x_i, x_j], axis=-1) * att[None]).sum(-1)
            alpha = jax.nn.leaky_relu(alpha, NEG_SLOPE)
            amax = jax.ops.segment_max(alpha, dst_f, num_segments=N)[dst_f]
            ex = jnp.exp(alpha - amax)
            denom = jax.ops.segment_sum(ex, dst_f, num_segments=N)[dst_f] + 1e-16
            a = ex / denom
            out = jax.ops.segment_sum(x_j * a[..., None], dst_f, num_segments=N)
            return out.mean(axis=1) + b
        N = x.shape[0]
        loop = jnp.arange(N, dtype=edge_index.dtype)
        src_f = jnp.concatenate([edge_index[0], loop])
        dst_f = jnp.concatenate([edge_index[1], loop])
        edge_attr_full = jnp.concatenate([edge_attr, jnp.zeros((N, edge_attr.shape[1]), edge_attr.dtype)], axis=0)
        h = x
        for l in range(N_LAYERS):
            h = _gat_layer(h, src_f, dst_f, edge_attr_full, weights[l], biases[l], edge_ws[l], edge_bs[l], atts[l])
            if l < N_LAYERS - 1:
                h = jax.nn.relu(h)
        return h
    edge_index = jnp.stack([src, dst])
    h = jnp.maximum(_layernorm(x, axis=-1), 0.0)
    x = x + _L0_gnn_ref(h, edge_index)
    h = jnp.maximum(_layernorm(x, axis=-1), 0.0)
    x = x + _L1_gnn_ref(h, L1_gnn_weight, edge_weight1, src, dst, edge_type_16)
    h = jnp.maximum(_layernorm(x, axis=-1), 0.0)
    x = x + _L2_gnn_ref(h, edge_index)
    h = jnp.maximum(_layernorm(x, axis=-1), 0.0)
    x = x + _L3_gnn_ref(h, edge_index, edge_attr_16, L3_gnn_weights, L3_gnn_biases, L3_gnn_edge_ws, L3_gnn_edge_bs, L3_gnn_atts)
    return x

_drawn_inputs = setup_inputs


def setup_inputs(seed=0):
    import zlib

    import numpy as np

    out = dict(_drawn_inputs(seed))
    spreads = {'L3_gnn_biases': (0.0, 0.8), 'L3_gnn_edge_bs': (0.0, 0.8)}
    factors = {'edge_attr_16': 8.0, 'L3_gnn_weights': 8.0, 'L3_gnn_edge_ws': 8.0, 'L3_gnn_atts': 8.0}
    for name, (base, spread) in spreads.items():
        noise = np.random.default_rng([zlib.crc32(name.encode()), seed]).standard_normal(out[name].shape)
        drawn = base * np.exp(spread * noise) if base else spread * noise
        out[name] = jnp.asarray(drawn.astype(out[name].dtype))
    for name, factor in factors.items():
        out[name] = (out[name] * factor).astype(out[name].dtype)
    return out
```

```python
from contextlib import ExitStack

import concourse.bass as bass
from concourse import mybir

ALU = mybir.AluOpType
ACT = mybir.ActivationFunctionType
AX_X = mybir.AxisListType.X
F32 = mybir.dt.float32
BF16 = mybir.dt.bfloat16
I32 = mybir.dt.int32

P = 128
G = 3
Q = 4
STEP_TILES = G * Q
RELS = 16
STEPS_L2 = 3
HEADS = 2
FEAT = 64
EDGE_F = 16
AW = FEAT + EDGE_F + 1
LN_EPS = 1e-5
LAMBDA_AMP = 0.1
GAMMA = 1.0 / (2.0 * (1.0 - LAMBDA_AMP))
FAR = -1.0e30
C_ONE, C_NORM, C_LOCAL, C_SRC, C_REL = EDGE_F, EDGE_F + 1, EDGE_F + 2, EDGE_F + 3, EDGE_F + 4
WA = EDGE_F + 5
B_LOCAL, B_DST = 0, 1
WB = 2


def sizes(nodes, edges):
    tiles = -(-edges // P)
    blocks = -(-nodes // P) + 1
    groups = (tiles * P + blocks * (G * P - 1)) // (G * P)
    steps = -(-groups // Q)
    steps += steps % 2
    return tiles, blocks, steps


def gnn_kernel(nc, nodes, x_in, src_in, dst_in, type_in, norm_in, attr_in, w1_in, wcat_in,
               wcatT_in, att_in, bias_in, out):
    T = src_in.shape[1]
    NBK = x_in.shape[1] // FEAT
    LAYERS = wcat_in.shape[0]
    KEY_PAD = (NBK - 1) * P
    _, _, STEPS = sizes(nodes, T * P)
    NG = STEPS * Q
    NT = NG * G
    NROW = NT * P
    CH = 31
    NCH = T // CH
    assert NCH * CH == T and NCH % 2 == 0

    sortedA = nc.dram_tensor("sortedA", (NROW, WA), F32, kind="Internal").ap()
    sortedB = nc.dram_tensor("sortedB", (NROW, WB), F32, kind="Internal").ap()
    table0 = nc.dram_tensor("table0", (NBK * P, FEAT + 1), F32, kind="Internal").ap()
    table1 = nc.dram_tensor("table1", (NBK * P * RELS, FEAT), F32, kind="Internal").ap()
    table2 = nc.dram_tensor("table2", (NBK * P, FEAT), F32, kind="Internal").ap()
    table3 = nc.dram_tensor("table3", (NBK * P, FEAT + HEADS), F32, kind="Internal").ap()

    with ExitStack() as ctx:
        def sb(name, shape, dt=F32):
            return ctx.enter_context(nc.sbuf_tensor(name, shape, dt))

        def sem(name):
            return ctx.enter_context(nc.semaphore(name))

        bank = [ctx.enter_context(nc.psum_tensor(f"bank{i}", [P, 512], F32)) for i in range(8)]

        SUM_BANK = [6, 7, 0, 1]

        iota_row = sb("iota_row", [P, P])
        ident = sb("ident", [P, P])
        identb = sb("identb", [P, P], BF16)
        before = sb("before", [P, P])
        ones = sb("ones", [P, P])
        group_no = sb("group_no", [P, NG])

        edgeA = sb("edgeA", [P, NT, WA])
        edgeB = sb("edgeB", [P, NT, WB])

        early = edgeA[:].rearrange("p t w -> p (t w)")
        taken = [0]

        def early_t(dt=F32):
            lo = taken[0]
            taken[0] += T
            assert taken[0] <= NT * WA
            return early[:, lo:lo + T] if dt is F32 else early[:, lo:lo + T].bitcast(dt)

        key_i = [early_t(I32) for s in range(2)]
        type_i = early_t(I32)
        part_i = early_t(I32)
        keyf = [early_t() for s in range(2)]
        norm_u = early_t()
        rel_u = early_t()
        block_of = early_t()
        local_of = [early_t() for s in range(2)]
        place = [early_t() for s in range(2)]
        member = early_t()
        running = early_t()
        offset = early_t()
        zeros_t = early_t()
        first_group = sb("first_group", [P, 1])
        first_row = sb("first_row", [P, 1])
        bucket_no = sb("bucket_no", [P, 1])
        count_f = sb("count_f", [P, 1])
        count_i = sb("count_i", [P, 1], I32)
        back_f = sb("back_f", [P, 1])
        over_f = sb("over_f", [P, 1])
        passed = sb("passed", [P, NG])
        block_f = [sb(f"block_f{s}", [P, NG]) for s in range(2)]
        block_i = [sb(f"block_i{s}", [P, NG], I32) for s in range(2)]
        chunkA = [sb(f"chunkA{c}", [P, CH, WA]) for c in range(2)]
        chunkB = [sb(f"chunkB{c}", [P, CH, WB]) for c in range(2)]
        chunk_at = [[sb(f"chunk_at{s}{c}", [P, CH], I32) for c in range(2)] for s in range(2)]
        fillA = sb("fillA", [P, 2 * STEP_TILES, WA])
        fillB = sb("fillB", [P, 2 * STEP_TILES, WB])
        FILLS = STEPS // 2

        x = sb("x", [P, NBK, FEAT])
        h = sb("h", [P, NBK, FEAT])
        hh = sb("hh", [P, NBK, FEAT])
        tmp = sb("tmp", [P, NBK, FEAT])
        dinv = sb("dinv", [P, NBK])
        nstat = [sb(f"nstat{i}", [P, NBK]) for i in range(3)]
        acc = sb("acc", [P, NBK * HEADS * AW])
        acc1 = acc[:, 0:NBK * (FEAT + 1)]
        acc1v = acc1.rearrange("p (b c) -> p b c", b=NBK)
        accv = acc[:].rearrange("p (b c) -> p b c", b=NBK * HEADS)

        gat_w = FEAT + HEADS
        rows = [sb(f"rows{p}", [P, STEP_TILES, gat_w]) for p in range(2)]
        at = [sb(f"at{p}", [P, STEP_TILES], I32) for p in range(2)]
        hot = [sb(f"hot{p}", [P, STEP_TILES, P]) for p in range(2)]

        w1 = sb("w1", [FEAT, RELS * FEAT])
        h_blk = sb("h_blk", [P, HEADS * AW])
        hT_blk = sb("hT_blk", [AW, HEADS, P])

        wcat = sb("wcat", [AW, HEADS * FEAT])
        wcatT = sb("wcatT", [FEAT, HEADS * AW])
        att = sb("att", [FEAT, 2 * HEADS])
        att_b = sb("att_b", [FEAT, 2 * HEADS, P])
        bias = sb("bias", [P, FEAT])
        vec = sb("vec", [P, 2 * HEADS, AW])
        tbl = sb("tbl", [P, NBK, gat_w])
        a_tgt = sb("a_tgt", [P, NBK * HEADS])
        a_max = sb("a_max", [P, NBK * HEADS])
        a_tmp = sb("a_tmp", [P, NBK * HEADS])
        far = sb("far", [P, STEP_TILES, P], BF16)
        hotT = sb("hotT", [P, STEP_TILES * P])
        scored = sb("scored", [P, Q, HEADS, G, P])
        y_blk = scored[:].rearrange("p q h j e -> p (q h j e)")[:, 0:RELS * FEAT]
        tgt_q = sb("tgt_q", [P, Q * HEADS])
        edge_p = sb("edge_p", [P, STEP_TILES, HEADS, EDGE_F + 1])
        edge_s = sb("edge_s", [P, STEP_TILES * HEADS])
        alpha = sb("alpha", [P, STEP_TILES * HEADS])
        argx = sb("argx", [P, STEP_TILES * HEADS])
        ex = sb("ex", [P, STEP_TILES * HEADS])
        gmax = sb("gmax", [P, Q * HEADS])
        newmax = sb("newmax", [P, Q * HEADS])
        drop = sb("drop", [P, Q * HEADS])
        keep = sb("keep", [P, Q * HEADS])
        val = sb("val", [P, STEP_TILES, HEADS, AW])

        s_in = sem("s_in")
        s_w1 = sem("s_w1")
        s_fill = sem("s_fill")
        s_attr = [sem(f"s_attr{c}") for c in range(2)]
        s_scat = [sem(f"s_scat{c}") for c in range(2)]
        s_edge = sem("s_edge")
        s_tab0 = sem("s_tab0")
        s_tab1 = sem("s_tab1")
        s_tab2 = sem("s_tab2")
        s_tab3 = sem("s_tab3")
        s_lw = sem("s_lw")
        s_out = sem("s_out")
        s_aside = sem("s_aside")
        s_aside_pe = sem("s_aside_pe")
        s_pool_c = sem("s_pool_c")
        s_const = sem("s_const")
        s_fillready = sem("s_fillready")
        s_member = sem("s_member")
        s_counts = sem("s_counts")
        s_chunk = sem("s_chunk")
        s_sqin = sem("s_sqin")
        s_sqout = sem("s_sqout")
        s_t0 = sem("s_t0")
        s_t2 = sem("s_t2")
        s_t3 = sem("s_t3")
        s_hblk = sem("s_hblk")
        s_hT = sem("s_hT")
        s_hTc = sem("s_hTc")
        s_y = sem("s_y")
        s_yc = sem("s_yc")
        s_yfree = sem("s_yfree")
        s_attb = sem("s_attb")
        s_vec = sem("s_vec")
        s_lwfree = sem("s_lwfree")
        s_fb = sem("s_fb")
        s_fT = sem("s_fT")
        s_fTc = sem("s_fTc")
        s_fo = sem("s_fo")
        s_done = sem("s_done")

        class Pass:
            def __init__(self, name):
                self.idx = sem(f"{name}_idx")
                self.landed = [sem(f"{name}_landed{p}") for p in range(2)]
                self.hot = sem(f"{name}_hot")
                self.summed = sem(f"{name}_summed")
                self.added = sem(f"{name}_added")

        pass0, pass1, pass2, pass3 = Pass("sum"), Pass("rel"), Pass("amp"), Pass("gat")
        g_tgt = sem("g_tgt")
        g_T = sem("g_T")
        g_Tc = sem("g_Tc")
        g_tgte = sem("g_tgte")
        g_scored = sem("g_scored")
        g_across = sem("g_across")
        g_maxed = sem("g_maxed")
        g_newmax = sem("g_newmax")
        g_keep = sem("g_keep")
        g_maxe = sem("g_maxe")
        g_arg = sem("g_arg")
        g_ex = sem("g_ex")
        g_val = sem("g_val")

        block = ctx.enter_context(nc.Block())

        @block.sync
        def _(sp):
            sp.dma_start(key_i[0][:], dst_in).then_inc(s_in, 16)
            sp.dma_start(key_i[1][:], src_in).then_inc(s_in, 16)
            sp.dma_start(type_i[:], type_in).then_inc(s_in, 16)
            sp.dma_start(norm_u[:], norm_in).then_inc(s_in, 16)
            sp.dma_start(x[:].rearrange("p b c -> p (b c)"), x_in).then_inc(s_in, 16)
            sp.dma_start(w1[:].rearrange("p n -> p n"), w1_in).then_inc(s_w1, 16)
            sp.wait_ge(s_fillready, 1)
            va = sortedA.rearrange("(p k r) w -> k p (r w)", p=P, k=FILLS)
            vb = sortedB.rearrange("(p k r) w -> k p (r w)", p=P, k=FILLS)
            for k in range(FILLS):
                sp.dma_start(va[k], fillA[:].rearrange("p r w -> p (r w)")).then_inc(s_fill, 16)
                sp.dma_start(vb[k], fillB[:].rearrange("p r w -> p (r w)")).then_inc(s_fill, 16)
            def load_attr(chunk, c):
                sp.dma_start(chunkA[c][:, :, 0:EDGE_F],
                             attr_in[:, bass.ds(chunk * (CH * EDGE_F), CH * EDGE_F)]
                             .rearrange("p (t f) -> p t f", f=EDGE_F)).then_inc(s_attr[c], 16)

            for c in range(2):
                load_attr(c, c)
            with sp.Fori(1, NCH // 2) as i:
                for c in range(2):
                    sp.wait_ge(s_scat[c], i * (16 * 2 * CH))
                    load_attr(i * 2 + c, c)
            for c in range(2):
                sp.wait_ge(s_scat[c], NCH // 2 * 16 * 2 * CH)
            sp.dma_start(edgeA[:].rearrange("p (g j) w -> p g (j w)", j=G),
                         sortedA.rearrange("(g p j) w -> p g (j w)", p=P, j=G)).then_inc(s_edge, 16)
            sp.dma_start(edgeB[:].rearrange("p (g j) w -> p g (j w)", j=G),
                         sortedB.rearrange("(g p j) w -> p g (j w)", p=P, j=G)).then_inc(s_edge, 16)
            sp.wait_ge(s_t0, 1)
            sp.dma_start(table0.rearrange("(b p) c -> p b c", p=P),
                         tbl[:, :, 0:FEAT + 1]).then_inc(s_tab0, 16)
            t1 = table1.rearrange("(n r) c -> n (r c)", r=RELS)
            sp.sem_inc(s_yfree, 1)
            with sp.Fori(0, NBK) as b:
                sp.wait_ge(s_yc, b * 2 + 2)
                sp.dma_start(t1[bass.ds(b * P, P), :], y_blk).then_inc(s_tab1, 16)
                sp.wait_ge(s_tab1, b * 16 + 16)
                sp.sem_inc(s_yfree, 1)
            with sp.Fori(0, STEPS_L2) as k:
                sp.wait_ge(s_t2, k + 1)
                sp.dma_start(table2.rearrange("(b p) c -> p b c", p=P), tmp[:]).then_inc(s_tab2, 16)
            with sp.Fori(0, LAYERS) as l:
                sp.wait_ge(s_lwfree, l + 1)
                for dst, src in ((wcat, wcat_in), (wcatT, wcatT_in), (att, att_in)):
                    sp.dma_start(dst[:], src[bass.ds(l, 1), :, :].rearrange("a k n -> (a k) n")).then_inc(s_lw, 16)
                sp.dma_start(bias[:], bias_in[bass.ds(l * P, P), :]).then_inc(s_lw, 16)
                sp.wait_ge(s_t3, l + 1)
                sp.dma_start(table3.rearrange("(b p) c -> p b c", p=P), tbl[:]).then_inc(s_tab3, 16)
            sp.wait_ge(s_done, 1)
            sp.dma_start(out, x[:].rearrange("p b c -> p (b c)")).then_inc(s_out, 16)
            sp.wait_ge(s_out, 16)

        @block.gpsimd
        def _(pool):
            nc.gpsimd.iota(iota_row[:], [[1, P]], base=0, channel_multiplier=0,
                           allow_small_or_imprecise_dtypes=True).then_inc(s_pool_c, 1)
            nc.gpsimd.iota(group_no[:], [[1, NG]], base=0, channel_multiplier=0,
                           allow_small_or_imprecise_dtypes=True).then_inc(s_pool_c, 1)
            nc.gpsimd.memset(ident[:], 0.0).then_inc(s_pool_c, 1)
            nc.gpsimd.memset(before[:], 1.0).then_inc(s_pool_c, 1)
            nc.gpsimd.memset(ones[:], 1.0).then_inc(s_pool_c, 1)
            pool.wait_ge(s_pool_c, 5)
            nc.gpsimd.affine_select(out=ident[:], in_=ident[:], compare_op=ALU.not_equal, fill=1.0,
                                    base=0, pattern=[[-1, P]], channel_multiplier=1).then_inc(s_const, 1)
            nc.gpsimd.affine_select(out=before[:], in_=before[:], compare_op=ALU.is_gt, fill=0.0,
                                    base=0, pattern=[[1, P]], channel_multiplier=-1).then_inc(s_const, 1)

            pool.wait_ge(s_fill, 16 * 2 * FILLS)
            with pool.Fori(0, NCH // 2) as i:
                for c in range(2):
                    pool.wait_ge(s_chunk, i * 2 + c + 1)
                    pool.wait_ge(s_attr[c], i * 16 + 16)
                    pool.sem_inc(s_aside, 1)
                    for t in range(CH):
                        nc.gpsimd.indirect_dma_start(
                            sortedA, bass.IndirectOffsetOnAxis(ap=chunk_at[0][c][:, t:t + 1], axis=0),
                            chunkA[c][:, t, :], None).then_inc(s_scat[c], 16)
                        nc.gpsimd.indirect_dma_start(
                            sortedB, bass.IndirectOffsetOnAxis(ap=chunk_at[1][c][:, t:t + 1], axis=0),
                            chunkB[c][:, t, :], None).then_inc(s_scat[c], 16)

            def gather(ps, table, width, edges, column, n, step, p):
                pool.wait_ge(ps.added, n * Q + 1)
                nc.gpsimd.tensor_copy(at[p][:], edges[:, bass.ds(step * STEP_TILES, STEP_TILES), column]
                                      ).then_inc(ps.idx, 1)
                pool.wait_ge(ps.idx, n + 1)
                pool.sem_inc(s_aside, 1)
                for t in range(STEP_TILES):
                    nc.gpsimd.indirect_dma_start(
                        rows[p][:, t, 0:width], None, table,
                        bass.IndirectOffsetOnAxis(ap=at[p][:, t:t + 1], axis=0)
                        ).then_inc(ps.landed[p], 16)

            def gathers(ps, table, width, edges, column, base):
                with pool.Fori(0, STEPS // 2) as i:
                    for p in range(2):
                        gather(ps, table, width, edges, column, base + i * 2 + p, i * 2 + p, p)

            pool.wait_ge(s_edge, 32)
            pool.wait_ge(s_tab0, 16)
            gathers(pass0, table0, FEAT + 1, edgeA, C_SRC, 0)
            pool.wait_ge(s_tab1, 16 * NBK)
            gathers(pass1, table1, FEAT, edgeA, C_REL, 0)
            with pool.Fori(0, STEPS_L2) as k:
                pool.wait_ge(s_tab2, k * 16 + 16)
                pool.sem_inc(s_aside, 1)
                gathers(pass2, table2, FEAT, edgeB, B_DST, k * STEPS)
            with pool.Fori(0, LAYERS) as l:
                pool.wait_ge(s_tab3, l * 16 + 16)
                pool.sem_inc(s_aside, 1)
                gathers(pass3, table3, gat_w, edgeA, C_SRC, l * STEPS)

        @block.tensor
        def _(pe):
            pe.wait_ge(s_const, 3)
            halves = [(0, 512), (512, T)]
            with pe.Fori(0, 2 * NBK) as b:
                pe.wait_ge(s_member, b + 1)
                for n, (lo, hi) in enumerate(halves):
                    nc.tensor.matmul(bank[n][:, 0:hi - lo], before[:], member[:, lo:hi], start=True, stop=True)
                    nc.tensor.matmul(bank[2 + n][:, 0:hi - lo], ones[:], member[:, lo:hi], start=True,
                                     stop=True).then_inc(s_counts, 1)

            def sums(ps, width, done):
                with pe.Fori(0, STEPS // 2) as i:
                    for p in range(2):
                        n = done * STEPS + i * 2 + p
                        turn = done * (STEPS // 2) + i
                        pe.wait_ge(ps.landed[p], turn * (16 * STEP_TILES) + 16 * STEP_TILES)
                        pe.wait_ge(ps.hot, n + 1)
                        for q in range(Q):
                            for j in range(G):
                                t = q * G + j
                                mm = nc.tensor.matmul(bank[q][:, 0:width], hot[p][:, t, :],
                                                      rows[p][:, t, 0:width], start=(j == 0),
                                                      stop=(j == G - 1))
                            mm.then_inc(ps.summed, 1)

            sums(pass0, FEAT + 1, 0)
            pe.wait_ge(s_w1, 16)
            with pe.Fori(0, NBK) as b:
                pe.wait_ge(s_hblk, b + 1)
                pe.sem_inc(s_aside_pe, 1)
                nc.tensor.transpose(bank[0][0:FEAT, 0:P], h_blk[:, 0:FEAT], ident[:]).then_inc(s_hT, 1)
                pe.wait_ge(s_hTc, b + 1)
                for n in range(2):
                    nc.tensor.matmul(bank[1 + n][:, :], hT_blk[0:FEAT, 0, :], w1[:, n * 512:(n + 1) * 512],
                                     start=True, stop=True).then_inc(s_y, 1)
            sums(pass1, FEAT, 0)
            with pe.Fori(0, STEPS_L2) as k:
                sums(pass2, FEAT, k)

            with pe.Fori(0, LAYERS) as l:
                pe.wait_ge(s_lw, l * 64 + 64)
                pe.wait_ge(s_attb, l + 1)
                for c in range(2 * HEADS):
                    hd = c % HEADS
                    mm = nc.tensor.matmul(bank[7][:, c * AW:(c + 1) * AW], att_b[:, c, :],
                                          wcatT[:, hd * AW:(hd + 1) * AW], start=True, stop=True)
                mm.then_inc(s_vec, 1)
                with pe.Fori(0, STEPS // 2) as i:
                    for p in range(2):
                        n = l * STEPS + i * 2 + p
                        k0 = n * Q
                        pe.wait_ge(pass3.hot, n + 1)
                        for q in range(Q):
                            if q >= 2:
                                pe.wait_ge(g_Tc, k0 + (q - 1))
                            for j in range(G):
                                tr = nc.tensor.transpose(bank[q % 2][:, j * P:(j + 1) * P],
                                                         hot[p][:, q * G + j, :], ident[:])
                            tr.then_inc(g_T, 1)
                        pe.wait_ge(g_tgt, n + 1)
                        for q in range(Q):
                            pe.wait_ge(g_Tc, k0 + (q + 1))
                            for j in range(G):
                                t = q * G + j
                                mm = nc.tensor.matmul(bank[4][:, t * 2:t * 2 + 2], hotT[:, t * P:(t + 1) * P],
                                                      tgt_q[:, q * 2:q * 2 + 2], start=True, stop=True)
                        mm.then_inc(g_tgte, 1)
                        for q in range(Q):
                            pe.wait_ge(g_scored, k0 + (q + 1))
                            pe.wait_ge(g_maxed, k0 + (q + 1))
                            for hd in range(HEADS):
                                for j in range(G):
                                    dst = bank[2 + hd][:, j * P:(j + 1) * P]
                                    nc.tensor.matmul(dst, scored[:, q, hd, j, :], ident[:], start=True, stop=False)
                                    mm = nc.tensor.matmul(dst, far[:, q * G + j, :], identb[:], start=False, stop=True)
                            mm.then_inc(g_across, 1)
                        pe.wait_ge(g_newmax, n + 1)
                        for q in range(Q):
                            for j in range(G):
                                t = q * G + j
                                mm = nc.tensor.matmul(bank[5][:, t * 2:t * 2 + 2], hotT[:, t * P:(t + 1) * P],
                                                      newmax[:, q * 2:q * 2 + 2], start=True, stop=True)
                        mm.then_inc(g_maxe, 1)
                        pe.wait_ge(g_val, n + 1)
                        for q in range(Q):
                            dst = bank[SUM_BANK[q]][:, 0:HEADS * AW]
                            for j in range(G):
                                mm = nc.tensor.matmul(dst, hot[p][:, q * G + j, :],
                                                      val[:, q * G + j, :, :].rearrange("p h c -> p (h c)"),
                                                      start=(j == 0), stop=(j == G - 1))
                            mm.then_inc(pass3.summed, 1)
                with pe.Fori(0, NBK) as b:
                    m = l * NBK + b
                    pe.wait_ge(s_fb, m + 1)
                    for hd in range(HEADS):
                        tr = nc.tensor.transpose(bank[hd][0:AW, 0:P], h_blk[:, hd * AW:(hd + 1) * AW], ident[:])
                    tr.then_inc(s_fT, 1)
                    pe.wait_ge(s_fTc, m + 1)
                    for hd in range(HEADS):
                        mm = nc.tensor.matmul(bank[2][:, 0:FEAT], hT_blk[:, hd, :], wcat[:, hd * FEAT:(hd + 1) * FEAT],
                                              start=(hd == 0), stop=(hd == HEADS - 1))
                    mm.then_inc(s_fo, 1)

        @block.scalar
        def _(act):
            def roots(ready):
                act.wait_ge(s_sqin, ready)
                nc.scalar.activation(nstat[1][:], nstat[0][:], ACT.Sqrt).then_inc(s_sqout, 1)
            roots(1)
            roots(2)
            roots(3)
            with act.Fori(0, NBK) as b:
                act.wait_ge(s_hT, b + 1)
                nc.scalar.copy(hT_blk[0:FEAT, 0, :], bank[0][0:FEAT, 0:P]).then_inc(s_hTc, 1)
                act.wait_ge(s_y, b * 2 + 1)
                act.wait_ge(s_yfree, b + 1)
                nc.scalar.copy(y_blk[:, 0:512], bank[1][:, :]).then_inc(s_yc, 1)
            roots(4)
            with act.Fori(0, STEPS_L2) as k:
                roots(k + 5)
            roots(5 + STEPS_L2)
            with act.Fori(0, LAYERS) as l:
                with act.Fori(0, STEPS // 2) as i:
                    for p in range(2):
                        n = l * STEPS + i * 2 + p
                        k0 = n * Q
                        for q in range(Q):
                            act.wait_ge(g_T, k0 + (q + 1))
                            nc.scalar.copy(hotT[:, q * G * P:(q + 1) * G * P], bank[q % 2][:, 0:G * P]
                                           ).then_inc(g_Tc, 1)
                        act.wait_ge(g_newmax, n + 1)
                        nc.scalar.activation(keep[:], drop[:], ACT.Exp).then_inc(g_keep, 1)
                        act.wait_ge(g_arg, n + 1)
                        nc.scalar.activation(ex[:], argx[:], ACT.Exp).then_inc(g_ex, 1)
                with act.Fori(0, NBK) as b:
                    m = l * NBK + b
                    act.wait_ge(s_fT, m + 1)
                    for hd in range(HEADS):
                        cp = nc.scalar.copy(hT_blk[:, hd, :], bank[hd][0:AW, 0:P])
                    cp.then_inc(s_fTc, 1)

        @block.vector
        def _(dve):
            V = nc.vector

            def wide(a, n):
                return a.unsqueeze(2).broadcast_to(list(a.shape) + [n])

            dve.wait_ge(s_const, 2)
            V.tensor_copy(identb[:], ident[:]).then_inc(s_const, 1)
            V.memset(fillA[:].rearrange("p r w -> p (r w)"), 0.0)
            V.memset(fillB[:].rearrange("p r w -> p (r w)"), 0.0)
            dve.drain()
            V.memset(fillA[:, :, C_LOCAL], -1.0)
            V.memset(fillB[:, :, B_LOCAL], -1.0)
            dve.drain()
            V.memset(first_group[:], 0.0).then_inc(s_fillready, 1)
            for c in range(2):
                V.memset(chunkA[c][:, :, C_ONE], 1.0)
            V.memset(zeros_t[:], 0.0)
            dve.wait_ge(s_in, 80)
            for s in range(2):
                V.tensor_copy(keyf[s][:], key_i[s][:])
            V.tensor_copy(rel_u[:], type_i[:])
            dve.drain()
            V.scalar_tensor_tensor(rel_u[:], keyf[1][:], float(RELS), rel_u[:], ALU.mult, ALU.add)

            for s in range(2):
                V.tensor_scalar(part_i[:], key_i[s][:], 7, None, ALU.arith_shift_right)
                dve.drain()
                V.tensor_copy(block_of[:], part_i[:])
                dve.drain()
                V.scalar_tensor_tensor(local_of[s][:], block_of[:], -float(P), keyf[s][:], ALU.mult, ALU.add)
                V.memset(place[s][:], 0.0)
                V.memset(first_group[:], 0.0)
                V.memset(bucket_no[:], 0.0)
                V.memset(block_f[s][:], 0.0)
                dve.drain()
                with dve.Fori(s * NBK, (s + 1) * NBK) as b:
                    V.tensor_scalar(member[:], block_of[:], bucket_no[:, 0:1], None, ALU.is_equal).then_inc(s_member, 1)
                    V.tensor_scalar(first_row[:], first_group[:], float(G * P), None, ALU.mult)
                    dve.wait_ge(s_counts, b * 2 + 2)
                    V.tensor_tensor_scan(running[:, 0:512], bank[2][:, :], zeros_t[:, 0:512], 0.0, ALU.add, ALU.add)
                    dve.drain()
                    V.tensor_tensor_scan(running[:, 512:T], bank[3][:, 0:T - 512], zeros_t[:, 512:T],
                                         running[:, 511:512], ALU.add, ALU.add)
                    dve.drain()
                    for n, (lo, hi) in enumerate([(0, 512), (512, T)]):
                        V.tensor_tensor(offset[:, lo:hi], running[:, lo:hi], bank[2 + n][:, 0:hi - lo], ALU.subtract)
                        dve.drain()
                        V.scalar_tensor_tensor(offset[:, lo:hi], offset[:, lo:hi], first_row[:, 0:1],
                                               bank[n][:, 0:hi - lo], ALU.add, ALU.add)
                    V.tensor_scalar(count_f[:], running[:, T - 1:T], 1.0 / (G * P), None, ALU.mult)
                    dve.drain()
                    V.tensor_tensor(offset[:], offset[:], member[:], ALU.mult)
                    V.tensor_copy(count_i[:], count_f[:])
                    dve.drain()
                    V.tensor_tensor(place[s][:], place[s][:], offset[:], ALU.add)
                    V.tensor_copy(back_f[:], count_i[:])
                    dve.drain()
                    V.tensor_scalar(over_f[:], back_f[:], float(G * P), None, ALU.mult)
                    dve.drain()
                    V.tensor_tensor(over_f[:], running[:, T - 1:T], over_f[:], ALU.is_gt)
                    V.tensor_tensor(first_group[:], first_group[:], back_f[:], ALU.add)
                    dve.drain()
                    V.tensor_tensor(first_group[:], first_group[:], over_f[:], ALU.add)
                    V.tensor_scalar(back_f[:], back_f[:], 1.0, float(G * P), ALU.subtract, ALU.mult)
                    dve.drain()
                    V.tensor_tensor(back_f[:], running[:, T - 1:T], back_f[:], ALU.is_le)
                    dve.drain()
                    V.tensor_tensor(first_group[:], first_group[:], back_f[:], ALU.subtract)
                    dve.drain()
                    V.tensor_scalar(passed[:], group_no[:], first_group[:, 0:1], None, ALU.is_ge)
                    V.tensor_scalar(bucket_no[:], bucket_no[:], 1.0, None, ALU.add)
                    dve.drain()
                    V.tensor_tensor(block_f[s][:], block_f[s][:], passed[:], ALU.add)
                    dve.drain()
                V.tensor_scalar(block_f[s][:], block_f[s][:], float(NBK - 1), None, ALU.min)
                dve.drain()
                V.tensor_copy(block_i[s][:], block_f[s][:])
                dve.drain()

            def chunk_rows(chunk, c):
                t = bass.ds(chunk * CH, CH)
                V.tensor_copy(chunkA[c][:, :, C_NORM], norm_u[:, t])
                V.tensor_copy(chunkA[c][:, :, C_LOCAL], local_of[0][:, t])
                V.tensor_copy(chunkA[c][:, :, C_SRC], keyf[1][:, t])
                V.tensor_copy(chunkA[c][:, :, C_REL], rel_u[:, t])
                V.tensor_copy(chunkB[c][:, :, B_LOCAL], local_of[1][:, t])
                V.tensor_copy(chunkB[c][:, :, B_DST], keyf[0][:, t])
                for s in range(2):
                    V.tensor_copy(chunk_at[s][c][:], place[s][:, t])
                dve.drain()
                dve.sem_inc(s_chunk, 1)

            for c in range(2):
                chunk_rows(c, c)
            with dve.Fori(1, NCH // 2) as i:
                for c in range(2):
                    dve.wait_ge(s_scat[c], i * (16 * 2 * CH))
                    chunk_rows(i * 2 + c, c)

            def root(values, ready):
                values().then_inc(s_sqin, 1)
                dve.wait_ge(s_sqout, ready)

            def layer_norm(ready):
                dve.drain()
                V.tensor_reduce(nstat[0][:], x[:], AX_X, ALU.add)
                dve.drain()
                V.tensor_scalar(nstat[2][:], nstat[0][:], 1.0 / FEAT, None, ALU.mult)
                dve.drain()
                V.tensor_tensor(h[:], x[:], wide(nstat[2][:], FEAT), ALU.subtract)
                dve.drain()
                V.tensor_tensor(tmp[:], h[:], h[:], ALU.mult)
                dve.drain()
                V.tensor_reduce(nstat[2][:], tmp[:], AX_X, ALU.add)
                dve.drain()
                root(lambda: V.tensor_scalar(nstat[0][:], nstat[2][:], 1.0 / FEAT, LN_EPS, ALU.mult, ALU.add), ready)
                V.reciprocal(nstat[2][:], nstat[1][:])
                dve.drain()
                V.tensor_tensor(h[:], h[:], wide(nstat[2][:], FEAT), ALU.mult)
                dve.drain()
                V.tensor_scalar(h[:], h[:], 0.0, None, ALU.max)
                dve.drain()

            def one_hots(edges, column, weight, step, p):
                for t in range(STEP_TILES):
                    at_edge = bass.ds(step * STEP_TILES + t, 1)
                    w = edges[:, at_edge, weight] if weight is not None else None
                    ins = V.tensor_scalar(hot[p][:, t, :], iota_row[:], edges[:, at_edge, column], w,
                                          ALU.is_equal, *([ALU.mult] if w is not None else []))
                return ins

            def blocks_of(s, step):
                return [dve.value_load(block_i[s][0:1, bass.ds(step * Q + q, 1)], min_val=0, max_val=NBK - 1)
                        for q in range(Q)]

            def add_pass(ps, s, edges, column, weight, width, base):
                V.memset(acc1, 0.0)
                dve.drain()
                view = acc1 if width == FEAT + 1 else acc[:, 0:NBK * width]
                with dve.Fori(0, STEPS // 2) as i:
                    for p in range(2):
                        step = i * 2 + p
                        n = base + i * 2 + p
                        one_hots(edges, column, weight, step, p).then_inc(ps.hot, 1)
                        blk = blocks_of(s, step)
                        for q in range(Q):
                            dve.wait_ge(ps.summed, n * Q + (q + 1))
                            a = view[:, bass.ds(blk[q] * width, width)]
                            V.tensor_tensor(a, a, bank[q][:, 0:width], ALU.add).then_inc(ps.added, 1)
                            dve.drain()

            for ps in (pass0, pass1, pass2, pass3):
                dve.sem_inc(ps.added, Q + 1)
            dve.sem_inc(g_maxed, 1)

            layer_norm(1)
            V.tensor_copy(tbl[:, :, 0:FEAT], h[:])
            V.memset(tbl[:, :, FEAT], 1.0)
            dve.drain()
            dve.sem_inc(s_t0, 1)
            dve.wait_ge(s_edge, 32)
            add_pass(pass0, 0, edgeA, C_LOCAL, None, FEAT + 1, 0)
            V.tensor_tensor(x[:], x[:], acc1v[:, :, 0:FEAT], ALU.add)
            root(lambda: V.tensor_scalar(nstat[0][:], acc1v[:, :, FEAT], 1.0, None, ALU.add), 2)
            V.reciprocal(dinv[:], nstat[1][:])

            layer_norm(3)
            with dve.Fori(0, NBK) as b:
                V.tensor_copy(h_blk[:, 0:FEAT], h[:, bass.ds(b, 1), :].rearrange("p a c -> p (a c)")).then_inc(s_hblk, 1)
                dve.wait_ge(s_y, b * 2 + 2)
                dve.wait_ge(s_yfree, b + 1)
                V.tensor_copy(y_blk[:, 512:1024], bank[2][:, :]).then_inc(s_yc, 1)
            add_pass(pass1, 0, edgeA, C_LOCAL, C_NORM, FEAT, 0)
            a1 = acc[:, 0:NBK * FEAT].rearrange("p (b c) -> p b c", c=FEAT)
            V.scalar_tensor_tensor(x[:], a1, 0.0, x[:], ALU.max, ALU.add)

            layer_norm(4)
            V.tensor_copy(hh[:], h[:])
            with dve.Fori(0, STEPS_L2) as k:
                dve.drain()
                V.tensor_tensor(tmp[:], h[:], wide(dinv[:], FEAT), ALU.mult)
                dve.drain()
                dve.sem_inc(s_t2, 1)
                add_pass(pass2, 1, edgeB, B_LOCAL, None, FEAT, k * STEPS)
                dve.wait_ge(s_tab2, k * 16 + 16)
                V.tensor_tensor(tmp[:], tmp[:], a1, ALU.add)
                dve.drain()
                V.tensor_tensor(tmp[:], tmp[:], wide(dinv[:], FEAT), ALU.mult)
                dve.drain()
                V.tensor_tensor(tmp[:], h[:], tmp[:], ALU.subtract)
                dve.drain()
                V.scalar_tensor_tensor(tmp[:], tmp[:], -GAMMA * 2.0 * (1.0 - LAMBDA_AMP), h[:], ALU.mult, ALU.add)
                dve.drain()
                V.tensor_tensor(tmp[:], tmp[:], hh[:], ALU.subtract)
                dve.drain()
                V.tensor_tensor(h[:], tmp[:], tmp[:], ALU.mult)
                dve.drain()
                V.tensor_reduce(nstat[2][:], h[:], AX_X, ALU.add)
                dve.drain()
                root(lambda: V.tensor_copy(nstat[0][:], nstat[2][:]), k + 5)
                V.tensor_scalar(nstat[2][:], nstat[1][:], 1e-30, None, ALU.max)
                V.tensor_scalar(nstat[0][:], nstat[1][:], GAMMA * LAMBDA_AMP, 0.0, ALU.subtract, ALU.max)
                dve.drain()
                V.reciprocal(nstat[2][:], nstat[2][:])
                dve.drain()
                V.tensor_tensor(nstat[0][:], nstat[0][:], nstat[2][:], ALU.mult)
                dve.drain()
                V.tensor_tensor(tmp[:], tmp[:], wide(nstat[0][:], FEAT), ALU.mult)
                dve.drain()
                V.tensor_tensor(h[:], hh[:], tmp[:], ALU.add)
            dve.drain()
            V.tensor_tensor(x[:], x[:], h[:], ALU.add)

            layer_norm(5 + STEPS_L2)
            dve.sem_inc(s_lwfree, 1)
            with dve.Fori(0, LAYERS) as l:
                V.tensor_scalar(h[:], h[:], 0.0, None, ALU.max)
                dve.wait_ge(s_lw, l * 64 + 64)
                V.tensor_copy(att_b[:], wide(att[:], P)).then_inc(s_attb, 1)
                dve.wait_ge(s_vec, l + 1)
                V.tensor_copy(vec[:].rearrange("p c k -> p (c k)"), bank[7][:, 0:2 * HEADS * AW])
                dve.drain()
                V.tensor_copy(tbl[:, :, 0:FEAT], h[:])
                tgt_v = a_tgt[:].rearrange("p (b h) -> p b h", h=HEADS)
                tmp_v = a_tmp[:].rearrange("p (b h) -> p b h", h=HEADS)
                for c in range(2 * HEADS):
                    w = vec[:, c:c + 1, 0:FEAT].broadcast_to([P, NBK, FEAT])
                    V.tensor_tensor(tmp[:], h[:], w, ALU.mult)
                    dve.drain()
                    dest = tbl[:, :, FEAT + c] if c < HEADS else tgt_v[:, :, c - HEADS]
                    V.tensor_reduce(dest, tmp[:], AX_X, ALU.add)
                    dve.drain()
                dve.sem_inc(s_t3, 1)
                V.tensor_tensor(tmp_v, tgt_v, tbl[:, :, FEAT:FEAT + HEADS], ALU.add)
                dve.drain()
                V.tensor_tensor(tmp_v, tmp_v, vec[:, 0:HEADS, AW - 1].unsqueeze(1).broadcast_to([P, NBK, HEADS]), ALU.add)
                V.memset(acc[:], 0.0)
                dve.drain()
                V.scalar_tensor_tensor(a_max[:], a_tmp[:], 0.2, a_tmp[:], ALU.mult, ALU.max)
                av = acc[:].rearrange("p (b h c) -> p b h c", h=HEADS, c=AW)
                for hd in range(HEADS):
                    V.tensor_copy(av[:, :, hd, 0:FEAT], h[:])
                V.memset(accv[:, :, AW - 1], 1.0)
                dve.drain()

                with dve.Fori(0, STEPS // 2) as i:
                    for p in range(2):
                        step = i * 2 + p
                        n = l * STEPS + i * 2 + p
                        one_hots(edgeA, C_LOCAL, None, step, p).then_inc(pass3.hot, 1)
                        blk = blocks_of(0, step)
                        for q in range(Q):
                            ins = V.tensor_copy(tgt_q[:, q * 2:q * 2 + 2], a_tgt[:, bass.ds(blk[q] * 2, 2)])
                        ins.then_inc(g_tgt, 1)
                        for t in range(STEP_TILES):
                            V.tensor_scalar(far[:, t, :], iota_row[:], edgeA[:, bass.ds(step * STEP_TILES + t, 1), C_LOCAL],
                                            FAR, ALU.not_equal, ALU.mult)
                        tiles = bass.ds(step * STEP_TILES, STEP_TILES)
                        at_e = edgeA[:, tiles, 0:EDGE_F + 1].unsqueeze(2).broadcast_to([P, STEP_TILES, HEADS, EDGE_F + 1])
                        av_e = vec[:, 0:HEADS, FEAT:AW].unsqueeze(1).broadcast_to([P, STEP_TILES, HEADS, EDGE_F + 1])
                        V.tensor_tensor(edge_p[:], at_e, av_e, ALU.mult)
                        dve.drain()
                        V.tensor_reduce(edge_s[:].rearrange("p (t h) -> p t h", h=HEADS), edge_p[:], AX_X, ALU.add)
                        dve.drain()
                        dve.wait_ge(pass3.landed[p], (l * (STEPS // 2) + i) * (16 * STEP_TILES) + 16 * STEP_TILES)
                        es = edge_s[:].rearrange("p (t h) -> p t h", h=HEADS)
                        V.tensor_tensor(es, es, rows[p][:, :, FEAT:FEAT + HEADS], ALU.add)
                        dve.drain()
                        dve.wait_ge(g_tgte, n + 1)
                        V.tensor_tensor(edge_s[:], edge_s[:], bank[4][:, 0:2 * STEP_TILES], ALU.add)
                        dve.drain()
                        V.scalar_tensor_tensor(alpha[:], edge_s[:], 0.2, edge_s[:], ALU.mult, ALU.max)
                        dve.drain()
                        for q in range(Q):
                            for hd in range(HEADS):
                                for j in range(G):
                                    t = q * G + j
                                    ins = V.tensor_scalar(scored[:, q, hd, j, :], hot[p][:, t, :],
                                                          alpha[:, t * 2 + hd:t * 2 + hd + 1], None, ALU.mult)
                            ins.then_inc(g_scored, 1)
                        for q in range(Q):
                            dve.wait_ge(g_across, n * Q + (q + 1))
                            for hd in range(HEADS):
                                ins = V.tensor_reduce(gmax[:, q * 2 + hd:q * 2 + hd + 1], bank[2 + hd][:, 0:G * P], AX_X, ALU.max)
                            ins.then_inc(g_maxed, 1)
                            dve.drain()
                            mx = a_max[:, bass.ds(blk[q] * 2, 2)]
                            cols = slice(q * 2, q * 2 + 2)
                            V.tensor_tensor(newmax[:, cols], mx, gmax[:, cols], ALU.max)
                            dve.drain()
                            V.tensor_tensor(drop[:, cols], mx, newmax[:, cols], ALU.subtract)
                            dve.drain()
                            ins = V.tensor_copy(mx, newmax[:, cols])
                            dve.drain()
                        dve.sem_inc(g_newmax, 1)
                        dve.wait_ge(g_maxe, n + 1)
                        V.tensor_tensor(argx[:], alpha[:], bank[5][:, 0:2 * STEP_TILES], ALU.subtract)
                        dve.drain()
                        V.tensor_scalar(argx[:], argx[:], 0.0, None, ALU.min).then_inc(g_arg, 1)
                        dve.wait_ge(g_ex, n + 1)
                        exv = ex[:].rearrange("p (t h) -> p t h", h=HEADS)
                        V.tensor_tensor(val[:, :, :, 0:FEAT],
                                        rows[p][:, :, 0:FEAT].unsqueeze(2).broadcast_to([P, STEP_TILES, HEADS, FEAT]),
                                        exv.unsqueeze(3).broadcast_to([P, STEP_TILES, HEADS, FEAT]), ALU.mult)
                        V.tensor_tensor(val[:, :, :, FEAT:AW], at_e,
                                        exv.unsqueeze(3).broadcast_to([P, STEP_TILES, HEADS, EDGE_F + 1]),
                                        ALU.mult)
                        dve.drain()
                        dve.sem_inc(g_val, 1)
                        dve.wait_ge(g_keep, n + 1)
                        for q in range(Q):
                            dve.wait_ge(pass3.summed, n * Q + (q + 1))
                            for hd in range(HEADS):
                                a = acc[:, bass.ds(blk[q] * (HEADS * AW) + hd * AW, AW)]
                                lo = hd * AW
                                ins = V.scalar_tensor_tensor(a, a, keep[:, q * 2 + hd:q * 2 + hd + 1],
                                                             bank[SUM_BANK[q]][:, lo:lo + AW], ALU.mult, ALU.add)
                            ins.then_inc(pass3.added, 1)
                            dve.drain()

                V.tensor_scalar(a_tmp[:], accv[:, :, AW - 1], 1e-16, None, ALU.add)
                dve.drain()
                V.reciprocal(a_tmp[:], a_tmp[:])
                dve.drain()
                V.tensor_scalar(a_tmp[:], a_tmp[:], 1.0 / HEADS, None, ALU.mult)
                dve.drain()
                V.tensor_tensor(accv, accv, wide(a_tmp[:], AW), ALU.mult)
                dve.drain()
                with dve.Fori(0, NBK) as b:
                    m = l * NBK + b
                    V.tensor_copy(h_blk[:], acc[:, bass.ds(b * (HEADS * AW), HEADS * AW)]).then_inc(s_fb, 1)
                    dve.wait_ge(s_fo, m + 1)
                    V.tensor_tensor(h[:, bass.ds(b, 1), :].rearrange("p a c -> p (a c)"), bank[2][:, 0:FEAT], bias[:], ALU.add)
                    dve.drain()
                dve.sem_inc(s_lwfree, 1)
            dve.drain()
            V.tensor_tensor(x[:], x[:], h[:], ALU.add).then_inc(s_done, 1)


def kernel(x, src, dst, edge_attr_16, edge_type_16, edge_weight1, L1_gnn_weight, L3_gnn_weights,
           L3_gnn_biases, L3_gnn_edge_ws, L3_gnn_edge_bs, L3_gnn_atts):
    import numpy as np
    import concourse.bacc as bacc
    from concourse.bass_utils import run_bass_kernel_spmd

    nodes, edges = x.shape[0], src.shape[0]
    tiles, blocks, _ = sizes(nodes, edges)
    pad = tiles * P - edges

    def by_tile(a, fill):
        a = np.asarray(a)
        a = np.concatenate([a, np.full((pad,) + a.shape[1:], fill, a.dtype)])
        return np.ascontiguousarray(a.reshape((tiles, P) + a.shape[1:]).swapaxes(0, 1).reshape(P, -1))

    xp = np.concatenate([np.asarray(x), np.zeros((blocks * P - nodes, FEAT), np.float32)])
    xp = np.ascontiguousarray(xp.reshape(blocks, P, FEAT).swapaxes(0, 1).reshape(P, -1))
    w = np.asarray(L3_gnn_weights)
    layers = w.shape[0]
    w = w.reshape(layers, FEAT, HEADS, FEAT).transpose(0, 2, 1, 3)
    ew = np.asarray(L3_gnn_edge_ws).reshape(layers, HEADS, FEAT, EDGE_F).transpose(0, 1, 3, 2)
    eb = np.asarray(L3_gnn_edge_bs).reshape(layers, HEADS, 1, FEAT)
    wcat = np.concatenate([w, ew, eb], axis=2)
    atts = np.asarray(L3_gnn_atts).reshape(layers, HEADS, 2, FEAT)
    pad_key = (blocks - 1) * P
    arrays = {
        "x_in": xp,
        "src_in": by_tile(src, pad_key),
        "dst_in": by_tile(dst, pad_key),
        "type_in": by_tile(edge_type_16, 0),
        "norm_in": by_tile(edge_weight1, 0),
        "attr_in": by_tile(edge_attr_16, 0),
        "w1_in": np.ascontiguousarray(np.asarray(L1_gnn_weight).transpose(1, 0, 2).reshape(FEAT, -1)),
        "wcat_in": np.ascontiguousarray(wcat.transpose(0, 2, 1, 3).reshape(layers, AW, -1)),
        "wcatT_in": np.ascontiguousarray(wcat.transpose(0, 3, 1, 2).reshape(layers, FEAT, -1)),
        "att_in": np.ascontiguousarray(atts[:, :, ::-1].transpose(0, 3, 2, 1).reshape(layers, FEAT, -1)),
        "bias_in": np.ascontiguousarray(np.broadcast_to(np.asarray(L3_gnn_biases)[:, None], (layers, P, FEAT)).reshape(-1, FEAT)),
    }
    nc = bacc.Bacc("TRN2", target_bir_lowering=False, num_devices=1)
    args = {n: nc.dram_tensor(n, a.shape, mybir.dt.from_np(a.dtype), kind="ExternalInput").ap()
            for n, a in arrays.items()}
    out = nc.dram_tensor("out", (P, blocks * FEAT), F32, kind="ExternalOutput").ap()
    gnn_kernel(nc, nodes, out=out, **args)
    r = run_bass_kernel_spmd(nc, [arrays], core_ids=[0])
    got = r.results[0]["out"].reshape(P, blocks, FEAT).swapaxes(0, 1).reshape(-1, FEAT)[:nodes]
    return np.ascontiguousarray(got)
```

```python
from contextlib import ExitStack

import concourse.bass as bass
from concourse import mybir

ALU = mybir.AluOpType
ACT = mybir.ActivationFunctionType
AX_X = mybir.AxisListType.X
F32 = mybir.dt.float32
BF16 = mybir.dt.bfloat16
I32 = mybir.dt.int32

P = 128
K = 4
Q = 3
SLOTS = K * Q
ACT_SLOTS = SLOTS // 3
RELS = 16
STEPS_L2 = 3
HEADS = 2
FEAT = 64
EDGE_F = 16
AW = FEAT + EDGE_F + 1
LN_EPS = 1e-5
LAMBDA_AMP = 0.1
GAMMA = 1.0 / (2.0 * (1.0 - LAMBDA_AMP))
FAR = -1.0e30
C_ONE, C_NORM, C_LOCAL, C_SRC, C_REL = EDGE_F, EDGE_F + 1, EDGE_F + 2, EDGE_F + 3, EDGE_F + 4
WA = EDGE_F + 5
B_LOCAL, B_DST = 0, 1
WB = 2


def sizes(nodes, edges):
    tiles = -(-edges // P)
    blocks = -(-nodes // P) + 1
    rows = (tiles * P + (K - 1) * (nodes + 1)) // K
    steps = (rows + blocks * (Q * P - 1)) // (Q * P)
    steps += steps % 2 + 2
    return tiles, blocks, steps


def gnn_kernel(nc, nodes, x_in, src_in, dst_in, type_in, norm_in, attr_in, w1_in, wcat_in,
               wcatT_in, att_in, bias_in, out):
    T = src_in.shape[1]
    NBK = x_in.shape[1] // FEAT
    LAYERS = wcat_in.shape[0]
    KEY_PAD = (NBK - 1) * P
    _, _, STEPS = sizes(nodes, T * P)
    NG = STEPS * Q
    NT = NG * K
    NROW = NT * P
    CH = 13
    NCH = T // CH
    assert NCH * CH == T and NCH % 2 == 0
    COPIES = 4
    PARTS = [(a, min(a + COPIES, CH)) for a in range(0, CH, COPIES)]

    sortedA = nc.dram_tensor("sortedA", (NROW, WA), F32, kind="Internal").ap()
    sortedB = nc.dram_tensor("sortedB", (NROW, WB), F32, kind="Internal").ap()
    table0 = nc.dram_tensor("table0", (NBK * P, FEAT), F32, kind="Internal").ap()
    table1 = nc.dram_tensor("table1", (NBK * P * RELS, FEAT), F32, kind="Internal").ap()
    table2 = nc.dram_tensor("table2", (NBK * P, FEAT), F32, kind="Internal").ap()
    table3 = nc.dram_tensor("table3", (NBK * P, FEAT + HEADS), F32, kind="Internal").ap()

    with ExitStack() as ctx:
        def sb(name, shape, dt=F32):
            return ctx.enter_context(nc.sbuf_tensor(name, shape, dt))

        def sem(name):
            return ctx.enter_context(nc.semaphore(name))

        bank = [ctx.enter_context(nc.psum_tensor(f"bank{i}", [P, 512], F32)) for i in range(8)]

        iota_row = sb("iota_row", [P, P])
        ident = sb("ident", [P, P])
        identb = sb("identb", [P, P], BF16)
        before = sb("before", [P, P])
        after = sb("after", [P, P])
        ones = sb("ones", [P, P])
        step_no = sb("step_no", [P, STEPS])

        edgeA = sb("edgeA", [P, NT, WA])
        edgeB = sb("edgeB", [P, NT, WB])

        early = edgeA[:].rearrange("p t w -> p (t w)")
        taken = [0]

        def early_t(dt=F32):
            lo = taken[0]
            taken[0] += T
            assert taken[0] <= NT * WA
            return early[:, lo:lo + T] if dt is F32 else early[:, lo:lo + T].bitcast(dt)

        key_i = [early_t(I32) for s in range(2)]
        type_i = early_t(I32)
        part_i = early_t(I32)
        keyf = [early_t() for s in range(2)]
        norm_u = early_t()
        rel_u = early_t()
        block_of = [early_t() for s in range(2)]
        local_of = [early_t() for s in range(2)]
        counts = [sb(f"counts{s}", [P, NBK]) for s in range(2)]
        rows_i = sb("rows_i", [P, NBK], I32)
        rows_f = sb("rows_f", [P, NBK])
        steps_i = sb("steps_i", [P, NBK], I32)
        steps_f = sb("steps_f", [P, NBK])
        steps_end = sb("steps_end", [P, NBK])
        spare_f = sb("spare_f", [P, NBK])
        zeros_b = sb("zeros_b", [P, NBK])
        first_slot = [sb(f"first_slot{s}", [P, NBK]) for s in range(2)]
        next_slot = [sb(f"next_slot{r}", [P, NBK]) for r in range(2)]
        block_f = sb("block_f", [P, STEPS])
        block_i = [sb(f"block_i{s}", [P, STEPS], I32) for s in range(2)]
        pairs_i = [sb(f"pairs_i{s}", [P, 1], I32) for s in range(2)]
        loc_c = [sb(f"loc_c{c}", [P, CH]) for c in range(2)]
        blk_c = [sb(f"blk_c{c}", [P, CH]) for c in range(2)]
        key_c = [sb(f"key_c{c}", [P, CH]) for c in range(2)]
        in_blk = [sb(f"in_blk{c}", [P, CH, NBK], BF16) for c in range(2)]
        rank = sb("rank", [P, CH])
        slot_p = sb("slot_p", [P, CH, NBK])
        slot_f = sb("slot_f", [P, CH])
        chunkA = [sb(f"chunkA{c}", [P, CH, WA]) for c in range(2)]
        chunkB = [sb(f"chunkB{c}", [P, CH, WB]) for c in range(2)]
        chunk_at = [sb(f"chunk_at{c}", [P, CH], I32) for c in range(2)]
        FILLS = STEPS // 2

        x = sb("x", [P, NBK, FEAT])
        h = sb("h", [P, NBK, FEAT])
        tmp = sb("tmp", [P, NBK, FEAT])
        dinv = sb("dinv", [P, NBK])
        nstat = [sb(f"nstat{i}", [P, NBK]) for i in range(3)]
        acc = sb("acc", [P, NBK * HEADS * AW])
        H2 = CH * P // 2
        in_loc = [acc[:, c * H2:(c + 1) * H2].bitcast(BF16).rearrange("p (t e) -> p t e", e=P) for c in range(2)]
        same = acc[:, 2 * H2:3 * H2].bitcast(BF16).rearrange("p (t e) -> p t e", e=P)
        locT = acc[:, 3 * H2:5 * H2]
        assert 5 * H2 <= NBK * HEADS * AW
        flat = tmp[:].rearrange("p b c -> p (b c)")
        fillA = flat[:, 0:2 * SLOTS * WA].rearrange("p (r w) -> p r w", w=WA)
        fillB = flat[:, 2 * SLOTS * WA:2 * SLOTS * (WA + WB)].rearrange("p (r w) -> p r w", w=WB)
        acc1 = acc[:, 0:NBK * FEAT]
        a1 = acc1.rearrange("p (b c) -> p b c", c=FEAT)
        accv = acc[:].rearrange("p (b c) -> p b c", b=NBK * HEADS)

        gat_w = FEAT + HEADS
        rows = [sb(f"rows{p}", [P, SLOTS, gat_w]) for p in range(2)]
        at = [sb(f"at{p}", [P, SLOTS], I32) for p in range(2)]
        hot = [sb(f"hot{p}", [P, Q, P]) for p in range(2)]
        row_loc = [sb(f"row_loc{s}", [P, NG]) for s in range(2)]
        empty = sb("empty", [P, NT])

        h_blk = [sb(f"h_blk{p}", [P, FEAT]) for p in range(2)]
        hT_blk = [sb(f"hT_blk{p}", [FEAT, P]) for p in range(2)]

        wcat = sb("wcat", [AW, HEADS * FEAT])
        wcatT = sb("wcatT", [FEAT, HEADS * AW])
        att = sb("att", [FEAT, 2 * HEADS])
        att_b = sb("att_b", [FEAT, 2 * HEADS, P])
        bias = sb("bias", [P, FEAT])
        edge_y = sb("edge_y", [P, 2 * RELS * FEAT])
        hh = edge_y[:, 0:NBK * FEAT].rearrange("p (b c) -> p b c", c=FEAT)
        scored = edge_y[:, 0:HEADS * Q * P].rearrange("p (h q e) -> p h q e", h=HEADS, q=Q)
        hotT = edge_y[:, HEADS * Q * P:(HEADS + 1) * Q * P]
        edge_p = edge_y[:, (HEADS + 1) * Q * P:(HEADS + 1) * Q * P + SLOTS * HEADS * (EDGE_F + 1)].rearrange(
            "p (t h f) -> p t h f", t=SLOTS, h=HEADS)
        vec = sb("vec", [P, 2 * HEADS, AW])
        tbl = sb("tbl", [P, NBK, gat_w])
        a_tgt = sb("a_tgt", [P, NBK * HEADS])
        a_max = sb("a_max", [P, NBK * HEADS])
        a_tmp = sb("a_tmp", [P, NBK * HEADS])
        far = sb("far", [P, Q, P])
        row_max = sb("row_max", [P, Q * HEADS])
        tgt_q = sb("tgt_q", [P, HEADS])
        edge_s = sb("edge_s", [P, SLOTS * HEADS])
        alpha = sb("alpha", [P, SLOTS * HEADS])
        argx = sb("argx", [P, SLOTS * HEADS])
        ex = sb("ex", [P, SLOTS * HEADS])
        gmax = sb("gmax", [P, HEADS])
        newmax = sb("newmax", [P, HEADS])
        drop = [sb(f"drop{p}", [P, HEADS]) for p in range(2)]
        keep = [sb(f"keep{p}", [P, HEADS]) for p in range(2)]
        val = sb("val", [P, SLOTS, HEADS, AW])
        FB = 2
        NF = NBK // FB
        assert NF * FB == NBK and NF % 2 == 1
        AG = FB * HEADS * AW
        val_f = val[:].rearrange("p t h c -> p (t h c)")
        agg = [val_f[:, p * AG:(p + 1) * AG].rearrange("p (c k) -> p c k", k=AW) for p in range(2)]
        aggT = val_f[0:AW, 2 * AG:2 * AG + FB * HEADS * P].rearrange("p (c e) -> p c e", e=P)
        w1 = val[0:FEAT].rearrange("p t h c -> p (t h c)")[:, 0:RELS * FEAT]
        y_blk = [edge_y[:, p * RELS * FEAT:(p + 1) * RELS * FEAT] for p in range(2)]

        s_in = sem("s_in")
        s_w1 = sem("s_w1")
        s_fill = sem("s_fill")
        s_attr = [sem(f"s_attr{c}") for c in range(2)]
        s_scat = [sem(f"s_scat{c}") for c in range(2)]
        s_edge = sem("s_edge")
        s_tab0 = sem("s_tab0")
        s_tab2 = sem("s_tab2")
        s_tab3 = sem("s_tab3")
        s_lw = sem("s_lw")
        s_out = sem("s_out")
        s_aside = sem("s_aside")
        s_aside_pe = sem("s_aside_pe")
        s_pool_c = sem("s_pool_c")
        s_const = sem("s_const")
        s_fillready = sem("s_fillready")
        s_onehot = sem("s_onehot")
        s_hist = sem("s_hist")
        s_rows = sem("s_rows")
        s_prefix = sem("s_prefix")
        s_first = sem("s_first")
        s_ready = sem("s_ready")
        s_locT = sem("s_locT")
        s_locTc = sem("s_locTc")
        s_keyrow = sem("s_keyrow")
        s_ranked = sem("s_ranked")
        s_taken = sem("s_taken")
        s_next = sem("s_next")
        s_chunk = sem("s_chunk")
        s_sqin = sem("s_sqin")
        s_sqout = sem("s_sqout")
        s_t0 = sem("s_t0")
        s_t2 = sem("s_t2")
        s_t3 = sem("s_t3")
        s_hblk = sem("s_hblk")
        s_hT = sem("s_hT")
        s_hTc = sem("s_hTc")
        s_y = sem("s_y")
        s_yc = sem("s_yc")
        s_yfree = sem("s_yfree")
        s_tab1 = [sem(f"s_tab1{p}") for p in range(2)]
        s_attb = sem("s_attb")
        s_vec = sem("s_vec")
        s_lwfree = sem("s_lwfree")
        s_fb = sem("s_fb")
        s_fT = sem("s_fT")
        s_fTc = sem("s_fTc")
        s_fo = sem("s_fo")
        s_done = sem("s_done")

        class Pass:
            def __init__(self, name):
                self.idx = sem(f"{name}_idx")
                self.landed = [sem(f"{name}_landed{p}") for p in range(2)]
                self.hot = sem(f"{name}_hot")
                self.summed = sem(f"{name}_summed")
                self.added = sem(f"{name}_added")

        pass0, pass1, pass2, pass3 = Pass("sum"), Pass("rel"), Pass("amp"), Pass("gat")
        g_tgt = sem("g_tgt")
        g_T = sem("g_T")
        g_Tc = sem("g_Tc")
        g_tgte = sem("g_tgte")
        g_scored = sem("g_scored")
        g_across = sem("g_across")
        g_newmax = sem("g_newmax")
        g_keep = sem("g_keep")
        g_maxe = sem("g_maxe")
        g_arg = sem("g_arg")
        g_ex = sem("g_ex")
        g_val = sem("g_val")
        g_valA = sem("g_valA")

        def pairs_of(eng, s):
            return eng.value_load(pairs_i[s][0:1, 0:1], min_val=1, max_val=STEPS // 2 - 1)

        block = ctx.enter_context(nc.Block())

        @block.sync
        def _(sp):
            sp.dma_start(key_i[0][:], dst_in).then_inc(s_in, 16)
            sp.dma_start(key_i[1][:], src_in).then_inc(s_in, 16)
            sp.dma_start(type_i[:], type_in).then_inc(s_in, 16)
            sp.dma_start(norm_u[:], norm_in).then_inc(s_in, 16)
            sp.dma_start(x[:].rearrange("p b c -> p (b c)"), x_in).then_inc(s_in, 16)
            sp.dma_start(w1, w1_in).then_inc(s_w1, 16)
            sp.wait_ge(s_fillready, 1)
            va = sortedA.rearrange("(p k r) w -> k p (r w)", p=P, k=FILLS)
            vb = sortedB.rearrange("(p k r) w -> k p (r w)", p=P, k=FILLS)
            for k in range(FILLS):
                sp.dma_start(va[k], flat[:, 0:2 * SLOTS * WA]).then_inc(s_fill, 16)
                sp.dma_start(vb[k], flat[:, 2 * SLOTS * WA:2 * SLOTS * (WA + WB)]).then_inc(s_fill, 16)
            def load_attr(chunk, c):
                sp.dma_start(chunkA[c][:, :, 0:EDGE_F],
                             attr_in[:, bass.ds(chunk * (CH * EDGE_F), CH * EDGE_F)]
                             .rearrange("p (t f) -> p t f", f=EDGE_F)).then_inc(s_attr[c], 16)

            for c in range(2):
                load_attr(c, c)
            with sp.Fori(1, NCH // 2) as i:
                for c in range(2):
                    sp.wait_ge(s_scat[c], i * (16 * CH))
                    load_attr(i * 2 + c, c)
            for c in range(2):
                sp.wait_ge(s_scat[c], NCH * 16 * CH)
            sp.dma_start(edgeA[:].rearrange("p (g j) w -> p g (j w)", j=K),
                         sortedA.rearrange("(g p j) w -> p g (j w)", p=P, j=K)).then_inc(s_edge, 16)
            sp.dma_start(edgeB[:].rearrange("p (g j) w -> p g (j w)", j=K),
                         sortedB.rearrange("(g p j) w -> p g (j w)", p=P, j=K)).then_inc(s_edge, 16)
            sp.wait_ge(s_t0, 1)
            sp.dma_start(table0.rearrange("(b p) c -> p b c", p=P),
                         tbl[:, :, 0:FEAT]).then_inc(s_tab0, 16)
            t1 = table1.rearrange("(n r) c -> n (r c)", r=RELS)
            sp.sem_inc(s_yfree, 2)
            with sp.Fori(0, NBK // 2) as i:
                for p in range(2):
                    sp.wait_ge(s_yc, i * 2 + (p + 1))
                    sp.dma_start(t1[bass.ds((i * 2 + p) * P, P), :], y_blk[p]).then_inc(s_tab1[p], 16)
                    sp.wait_ge(s_tab1[p], i * 16 + 16)
                    sp.sem_inc(s_yfree, 1)
            with sp.Fori(0, STEPS_L2) as k:
                sp.wait_ge(s_t2, k + 1)
                sp.dma_start(table2.rearrange("(b p) c -> p b c", p=P), tmp[:]).then_inc(s_tab2, 16)
            with sp.Fori(0, LAYERS) as l:
                sp.wait_ge(s_lwfree, l + 1)
                for dst, src in ((wcat, wcat_in), (wcatT, wcatT_in), (att, att_in)):
                    sp.dma_start(dst[:], src[bass.ds(l, 1), :, :].rearrange("a k n -> (a k) n")).then_inc(s_lw, 16)
                sp.dma_start(bias[:], bias_in[bass.ds(l * P, P), :]).then_inc(s_lw, 16)
                sp.wait_ge(s_t3, l + 1)
                sp.dma_start(table3.rearrange("(b p) c -> p b c", p=P), tbl[:]).then_inc(s_tab3, 16)
            sp.wait_ge(s_done, 1)
            sp.dma_start(out, x[:].rearrange("p b c -> p (b c)")).then_inc(s_out, 16)
            sp.wait_ge(s_out, 16)

        @block.gpsimd
        def _(pool):
            nc.gpsimd.iota(iota_row[:], [[1, P]], base=0, channel_multiplier=0,
                           allow_small_or_imprecise_dtypes=True).then_inc(s_pool_c, 1)
            nc.gpsimd.iota(step_no[:], [[1, STEPS]], base=0, channel_multiplier=0,
                           allow_small_or_imprecise_dtypes=True).then_inc(s_pool_c, 1)
            nc.gpsimd.memset(ident[:], 0.0).then_inc(s_pool_c, 1)
            nc.gpsimd.memset(before[:], 1.0).then_inc(s_pool_c, 1)
            nc.gpsimd.memset(after[:], 1.0).then_inc(s_pool_c, 1)
            nc.gpsimd.memset(ones[:], 1.0).then_inc(s_pool_c, 1)
            pool.wait_ge(s_pool_c, 6)
            nc.gpsimd.affine_select(out=ident[:], in_=ident[:], compare_op=ALU.not_equal, fill=1.0,
                                    base=0, pattern=[[-1, P]], channel_multiplier=1).then_inc(s_const, 1)
            nc.gpsimd.affine_select(out=before[:], in_=before[:], compare_op=ALU.is_gt, fill=0.0,
                                    base=0, pattern=[[1, P]], channel_multiplier=-1).then_inc(s_const, 1)
            nc.gpsimd.affine_select(out=after[:], in_=after[:], compare_op=ALU.is_gt, fill=0.0,
                                    base=0, pattern=[[-1, P]], channel_multiplier=1).then_inc(s_const, 1)

            pool.wait_ge(s_fill, 16 * 2 * FILLS)
            def scatter(table, chunk, c, turn):
                for t in range(CH):
                    nc.gpsimd.indirect_dma_start(
                        table, bass.IndirectOffsetOnAxis(ap=chunk_at[c][:, t:t + 1], axis=0),
                        chunk[c][:, t, :], None).then_inc(s_scat[c], 16)

            for s, (table, chunk) in enumerate(((sortedA, chunkA), (sortedB, chunkB))):
                with pool.Fori(0, NCH // 2) as i:
                    for c in range(2):
                        pool.wait_ge(s_chunk, i * 2 + (s * NCH + c + 1))
                        if s == 0:
                            pool.wait_ge(s_attr[c], i * 16 + 16)
                        pool.sem_inc(s_aside, 1)
                        scatter(table, chunk, c, i)

            def gather(ps, table, width, edges, column, number, step, p):
                nc.gpsimd.tensor_copy(at[p][:], edges[:, bass.ds(step * SLOTS, SLOTS), column]
                                      ).then_inc(ps.idx, 1)
                pool.wait_ge(ps.idx, number + 1)
                pool.sem_inc(s_aside, 1)
                for t in range(SLOTS):
                    nc.gpsimd.indirect_dma_start(
                        rows[p][:, t, 0:width], None, table,
                        bass.IndirectOffsetOnAxis(ap=at[p][:, t:t + 1], axis=0)
                        ).then_inc(ps.landed[p], 16)

            def gathers(ps, table, width, edges, column, pairs, done):
                with pool.Fori(0, pairs) as i:
                    for p in range(2):
                        n = done * pairs * 2 + i * 2 + p
                        pool.wait_ge(ps.added, n + 1)
                        gather(ps, table, width, edges, column, n, i * 2 + p, p)

            pool.wait_ge(s_edge, 32)
            pairsA, pairsB = pairs_of(pool, 0), pairs_of(pool, 1)
            pool.wait_ge(s_tab0, 16)
            gathers(pass0, table0, FEAT, edgeA, C_SRC, pairsA, 0)
            for p in range(2):
                pool.wait_ge(s_tab1[p], 16 * (NBK // 2))
            gathers(pass1, table1, FEAT, edgeA, C_REL, pairsA, 0)
            with pool.Fori(0, STEPS_L2) as k:
                pool.wait_ge(s_tab2, k * 16 + 16)
                pool.sem_inc(s_aside, 1)
                gathers(pass2, table2, FEAT, edgeB, B_DST, pairsB, k)
            with pool.Fori(0, LAYERS) as l:
                pool.wait_ge(s_tab3, l * 16 + 16)
                pool.sem_inc(s_aside, 1)
                gather(pass3, table3, gat_w, edgeA, C_SRC, l * (pairsA * 2 + 1), 0, 0)
                with pool.Fori(0, pairsA) as i:
                    for p in range(2):
                        n = l * pairsA * 2 + i * 2 + p
                        pool.wait_ge(g_val, n + 1)
                        pool.wait_ge(g_valA, n + 1)
                        gather(pass3, table3, gat_w, edgeA, C_SRC, l * (pairsA * 2 + 1) + i * 2 + (p + 1),
                               i * 2 + (p + 1), 1 - p)

        @block.tensor
        def _(pe):
            pe.wait_ge(s_const, 4)
            pe.wait_ge(s_fillready, 1)
            for s in range(2):
                nc.tensor.matmul(bank[s][:, 0:NBK], ident[:], zeros_b[:], start=True, stop=False,
                                 skip_group_check=True)
                with pe.Fori(0, NCH // 2) as i:
                    for c in range(2):
                        pe.wait_ge(s_onehot, i * 2 + (s * NCH + c + 1))
                        for t in range(CH):
                            mm = nc.tensor.matmul(bank[s][:, 0:NBK], in_loc[c][:, t, :], in_blk[c][:, t, :],
                                                  start=False, stop=False, skip_group_check=True)
                        mm.then_inc(s_hist, 1)
            for s in range(2):
                pe.wait_ge(s_rows, s + 1)
                nc.tensor.matmul(bank[2][:, 0:NBK], before[:], rows_f[:], start=True, stop=True)
                nc.tensor.matmul(bank[3][:, 0:NBK], ones[:], rows_f[:], start=True, stop=True).then_inc(s_prefix, 1)
            for s in range(2):
                pe.wait_ge(s_first, s + 1)
                if s == 1:
                    pe.wait_ge(s_next, T + 1)
                nc.tensor.matmul(bank[5][:, 0:NBK], ident[:], first_slot[s][:], start=True, stop=False,
                                 skip_group_check=True).then_inc(s_taken, 1)
                with pe.Fori(0, NCH // 2) as i:
                    for c in range(2):
                        chunk = i * 2 + (s * NCH + c)
                        pe.wait_ge(s_onehot, chunk + (2 * NCH + 1))
                        for n, (a, z) in enumerate(PARTS):
                            part = chunk * len(PARTS) + n
                            pe.wait_ge(s_locTc, part + 1)
                            for t in range(a, z):
                                mm = nc.tensor.matmul(bank[n % 2][:, (t - a) * P:(t - a + 1) * P],
                                                      in_loc[c][:, t, :], identb[:], start=True, stop=True)
                            mm.then_inc(s_locT, 1)
                            pe.wait_ge(s_ranked, part + 1)
                            for t in range(a, z):
                                mm = nc.tensor.matmul(bank[2 + n % 2][:, (t - a) * P:(t - a + 1) * P],
                                                      key_c[c][:, t:t + 1].broadcast_to([P, P]), ident[:],
                                                      start=True, stop=True)
                            mm.then_inc(s_keyrow, 1)
                        for t in range(CH):
                            r = (c * CH + t) % 2
                            if t % COPIES == 0:
                                pe.wait_ge(s_locTc, chunk * len(PARTS) + (t // COPIES + 3))
                            pe.wait_ge(s_next, chunk * CH + (s + t + 1))
                            nc.tensor.matmul(bank[4][:, t * NBK:(t + 1) * NBK], locT[:, t * P:(t + 1) * P],
                                             next_slot[r][:], start=True, stop=True)
                            nc.tensor.matmul(bank[5][:, 0:NBK], in_loc[c][:, t, :], in_blk[c][:, t, :],
                                             start=False, stop=False, skip_group_check=True).then_inc(s_taken, 1)

            def sums(ps, pairs, done):
                with pe.Fori(0, pairs) as i:
                    for p in range(2):
                        n = done * pairs * 2 + i * 2 + p
                        pe.wait_ge(ps.landed[p], (done * pairs + i + 1) * (16 * SLOTS))
                        pe.wait_ge(ps.hot, n + 1)
                        for q in range(Q):
                            for j in range(K):
                                mm = nc.tensor.matmul(bank[p][:, 0:FEAT], hot[p][:, q, :],
                                                      rows[p][:, q * K + j, 0:FEAT],
                                                      start=(q + j == 0), stop=(q == Q - 1 and j == K - 1))
                        mm.then_inc(ps.summed, 1)

            pe.wait_ge(s_first, 2)
            pairsA, pairsB = pairs_of(pe, 0), pairs_of(pe, 1)
            sums(pass0, pairsA, 0)
            pe.wait_ge(s_w1, 16)
            with pe.Fori(0, NBK // 2) as i:
                for p in range(2):
                    b = i * 2 + p
                    pe.wait_ge(s_hblk, b + 1)
                    pe.sem_inc(s_aside_pe, 1)
                    nc.tensor.transpose(bank[p][0:FEAT, 0:P], h_blk[p][:], ident[:]).then_inc(s_hT, 1)
                    pe.wait_ge(s_hTc, b + 1)
                    for half in range(2):
                        nc.tensor.matmul(bank[2 + 2 * p + half][:, :], hT_blk[p][:], w1[:, half * 512:(half + 1) * 512],
                                         start=True, stop=True).then_inc(s_y, 1)
            sums(pass1, pairsA, 0)
            with pe.Fori(0, STEPS_L2) as k:
                sums(pass2, pairsB, k)

            def targets(number, p):
                pe.wait_ge(pass3.hot, number + 1)
                for q in range(Q):
                    tr = nc.tensor.transpose(bank[0][:, q * P:(q + 1) * P], hot[p][:, q, :], ident[:])
                tr.then_inc(g_T, 1)
                pe.wait_ge(g_Tc, number + 1)
                for q in range(Q):
                    mm = nc.tensor.matmul(bank[4][:, q * 2:q * 2 + 2], hotT[:, q * P:(q + 1) * P],
                                          tgt_q[:], start=True, stop=True)
                mm.then_inc(g_tgte, 1)

            def across(number):
                for hd in range(HEADS):
                    pe.wait_ge(g_scored, number * HEADS + (hd + 1))
                    for q in range(Q):
                        dst = bank[2 + hd][:, q * P:(q + 1) * P]
                        mm = nc.tensor.transpose(dst, scored[:, hd, q, :], ident[:])
                    mm.then_inc(g_across, 1)

            def maxima(number):
                pe.wait_ge(g_newmax, number + 1)
                for q in range(Q):
                    mm = nc.tensor.matmul(bank[5][:, q * 2:q * 2 + 2], hotT[:, q * P:(q + 1) * P],
                                          newmax[:], start=True, stop=True)
                mm.then_inc(g_maxe, 1)

            with pe.Fori(0, LAYERS) as l:
                pe.wait_ge(s_lw, l * 64 + 64)
                pe.wait_ge(s_attb, l + 1)
                for c in range(2 * HEADS):
                    hd = c % HEADS
                    mm = nc.tensor.matmul(bank[7][:, c * AW:(c + 1) * AW], att_b[:, c, :],
                                          wcatT[:, hd * AW:(hd + 1) * AW], start=True, stop=True)
                mm.then_inc(s_vec, 1)
                targets(l * (pairsA * 2 + 1), 0)
                across(l * (pairsA * 2 + 1))
                maxima(l * (pairsA * 2 + 1))
                with pe.Fori(0, pairsA) as i:
                    for p in range(2):
                        n = l * pairsA * 2 + i * 2 + p
                        ahead = l * (pairsA * 2 + 1) + i * 2 + (p + 1)
                        targets(ahead, 1 - p)
                        pe.wait_ge(g_val, n + 2)
                        pe.wait_ge(g_valA, n + 2)
                        for q in range(Q):
                            for j in range(K):
                                mm = nc.tensor.matmul(bank[6 + p][:, 0:HEADS * AW], hot[p][:, q, :],
                                                      val[:, q * K + j, :, :].rearrange("p h c -> p (h c)"),
                                                      start=(q + j == 0), stop=(q == Q - 1 and j == K - 1))
                        mm.then_inc(pass3.summed, 1)
                        across(ahead)
                        maxima(ahead)

                def through(m, p):
                    pe.wait_ge(s_fb, m + 1)
                    for c in range(FB * HEADS):
                        tr = nc.tensor.transpose(bank[p][0:AW, c * P:(c + 1) * P], agg[p][:, c, :], ident[:])
                    tr.then_inc(s_fT, 1)
                    pe.wait_ge(s_fTc, m + 1)
                    for c in range(FB):
                        for hd in range(HEADS):
                            mm = nc.tensor.matmul(bank[2 + p][:, c * FEAT:(c + 1) * FEAT], aggT[:, c * HEADS + hd, :],
                                                  wcat[:, hd * FEAT:(hd + 1) * FEAT],
                                                  start=(hd == 0), stop=(hd == HEADS - 1))
                    mm.then_inc(s_fo, 1)

                through(l * NF, 0)
                with pe.Fori(0, NF // 2) as b:
                    for p in range(2):
                        through(l * NF + b * 2 + (p + 1), 1 - p)

        @block.scalar
        def _(act):
            act.sem_inc(s_locTc, 2)
            for s in range(2):
                act.wait_ge(s_first, s + 1)
                act.wait_ge(s_taken, s * (T + 1) + 1)
                nc.scalar.copy(next_slot[0][:], bank[5][:, 0:NBK]).then_inc(s_next, 1)
                with act.Fori(0, NCH // 2) as i:
                    for c in range(2):
                        chunk = i * 2 + (s * NCH + c)
                        for n, (a, z) in enumerate(PARTS):
                            act.wait_ge(s_locT, chunk * len(PARTS) + (n + 1))
                            nc.scalar.copy(locT[:, a * P:z * P], bank[n % 2][:, 0:(z - a) * P]).then_inc(s_locTc, 1)
                        for t in range(CH):
                            act.wait_ge(s_taken, chunk * CH + (s + t + 2))
                            nc.scalar.copy(next_slot[(c * CH + t + 1) % 2][:], bank[5][:, 0:NBK]).then_inc(s_next, 1)

            def roots(ready):
                act.wait_ge(s_sqin, ready)
                nc.scalar.activation(nstat[1][:], nstat[0][:], ACT.Sqrt).then_inc(s_sqout, 1)
            roots(1)
            roots(2)
            roots(3)
            with act.Fori(0, NBK // 2) as i:
                for p in range(2):
                    b = i * 2 + p
                    act.wait_ge(s_hT, b + 3)
                    nc.scalar.copy(hT_blk[p][:], bank[p][0:FEAT, 0:P]).then_inc(s_hTc, 1)
                    act.wait_ge(s_y, b * 2 + 2)
                    act.wait_ge(s_yfree, b + 1)
                    for half in range(2):
                        cp = nc.scalar.copy(y_blk[p][:, half * 512:(half + 1) * 512], bank[2 + 2 * p + half][:, :])
                    cp.then_inc(s_yc, 1)
            roots(4)
            with act.Fori(0, STEPS_L2) as k:
                roots(k + 5)
            roots(5 + STEPS_L2)

            act.wait_ge(s_first, 2)
            pairsA = pairs_of(act, 0)

            def transposed(number):
                act.wait_ge(g_T, number + 1)
                nc.scalar.copy(hotT, bank[0][:, 0:Q * P]).then_inc(g_Tc, 1)

            def exponentials(number, p):
                act.wait_ge(g_newmax, number + 1)
                nc.scalar.activation(keep[p][:], drop[p][:], ACT.Exp).then_inc(g_keep, 1)
                act.wait_ge(g_arg, number + 1)
                nc.scalar.activation(ex[:], argx[:], ACT.Exp).then_inc(g_ex, 1)

            with act.Fori(0, LAYERS) as l:
                transposed(l * (pairsA * 2 + 1))
                exponentials(l * (pairsA * 2 + 1), 0)
                with act.Fori(0, pairsA) as i:
                    for p in range(2):
                        n = l * pairsA * 2 + i * 2 + p
                        ahead = l * (pairsA * 2 + 1) + i * 2 + (p + 1)
                        transposed(ahead)
                        act.wait_ge(g_ex, ahead)
                        act.wait_ge(pass3.summed, n + 1)
                        for t in range(ACT_SLOTS):
                            ins = nc.scalar.activation(val[:, t, 1, 0:FEAT], rows[p][:, t, 0:FEAT], ACT.Copy,
                                                       scale=ex[:, t * HEADS + 1:t * HEADS + 2])
                        ins.then_inc(g_valA, 1)
                        exponentials(ahead, 1 - p)

                def transposed_agg(m, p):
                    act.wait_ge(s_fT, m + 1)
                    nc.scalar.copy(aggT.rearrange("p c e -> p (c e)"), bank[p][0:AW, :]).then_inc(s_fTc, 1)

                transposed_agg(l * NF, 0)
                with act.Fori(0, NF // 2) as b:
                    for p in range(2):
                        transposed_agg(l * NF + b * 2 + (p + 1), 1 - p)

        @block.vector
        def _(dve):
            V = nc.vector

            def wide(a, n):
                return a.unsqueeze(2).broadcast_to(list(a.shape) + [n])

            dve.wait_ge(s_const, 3)
            V.tensor_copy(identb[:], ident[:]).then_inc(s_const, 1)
            V.memset(flat[:, 0:2 * SLOTS * WA], 0.0)
            V.memset(zeros_b[:], 0.0)
            dve.drain()
            V.memset(fillA[:, :, C_LOCAL], -1.0)
            V.memset(fillA[:, :, C_SRC], float(KEY_PAD))
            V.memset(fillA[:, :, C_REL], float(KEY_PAD * RELS))
            V.memset(fillB[:, :, B_LOCAL], -1.0)
            V.memset(fillB[:, :, B_DST], float(KEY_PAD))
            dve.drain()
            dve.sem_inc(s_fillready, 1)
            for c in range(2):
                V.memset(chunkA[c][:, :, C_ONE], 1.0)
            dve.wait_ge(s_in, 80)
            for s in range(2):
                V.tensor_copy(keyf[s][:], key_i[s][:])
            V.tensor_copy(rel_u[:], type_i[:])
            dve.drain()
            V.scalar_tensor_tensor(rel_u[:], keyf[1][:], float(RELS), rel_u[:], ALU.mult, ALU.add)
            for s in range(2):
                V.tensor_scalar(part_i[:], key_i[s][:], 7, None, ALU.arith_shift_right)
                dve.drain()
                V.tensor_copy(block_of[s][:], part_i[:])
                dve.drain()
                V.scalar_tensor_tensor(local_of[s][:], block_of[s][:], -float(P), keyf[s][:], ALU.mult, ALU.add)
            dve.drain()

            def chunk_hots(s, chunk, c):
                t = bass.ds(chunk * CH, CH)
                V.tensor_copy(loc_c[c][:], local_of[s][:, t])
                V.tensor_copy(blk_c[c][:], block_of[s][:, t])
                V.tensor_copy(key_c[c][:], keyf[s][:, t])
                dve.drain()
                for n in range(CH):
                    V.tensor_scalar(in_loc[c][:, n, :], iota_row[:], loc_c[c][:, n:n + 1], None, ALU.is_equal)
                V.tensor_tensor(in_blk[c][:], iota_row[:, 0:NBK].unsqueeze(1).broadcast_to([P, CH, NBK]),
                                wide(blk_c[c][:], NBK), ALU.is_equal)
                dve.drain()
                dve.sem_inc(s_onehot, 1)

            for s in range(2):
                for c in range(2):
                    if s == 1:
                        dve.wait_ge(s_hist, NCH - 1 + c)
                    chunk_hots(s, c, c)
                with dve.Fori(1, NCH // 2) as i:
                    for c in range(2):
                        dve.wait_ge(s_hist, i * 2 + (s * NCH + c - 1))
                        chunk_hots(s, i * 2 + c, c)
            dve.wait_ge(s_hist, 2 * NCH)
            for s in range(2):
                V.tensor_copy(counts[s][:], bank[s][:, 0:NBK])
            dve.drain()
            for s in range(2):
                V.tensor_copy(rows_i[:], counts[s][:])
                dve.drain()
                V.tensor_scalar(rows_f[:], counts[s][:], float(K - 1), None, ALU.add)
                dve.drain()
                V.tensor_copy(rows_i[:], rows_f[:])
                dve.drain()
                V.tensor_scalar(rows_i[:], rows_i[:], K.bit_length() - 1, None, ALU.arith_shift_right)
                dve.drain()
                V.tensor_copy(rows_f[:], rows_i[:])
                dve.drain()
                dve.sem_inc(s_rows, 1)
                dve.wait_ge(s_prefix, s + 1)
                V.tensor_scalar(steps_f[:], bank[3][:, 0:NBK], float(P * Q - 1), 1.0 / (P * Q), ALU.add, ALU.mult)
                V.tensor_scalar(steps_end[:], bank[3][:, 0:NBK], 1.0, None, ALU.mult)
                dve.drain()
                V.tensor_copy(steps_i[:], steps_f[:])
                dve.drain()
                V.tensor_copy(steps_f[:], steps_i[:])
                dve.drain()
                V.tensor_scalar(rows_f[:], steps_f[:], 1.0, float(P * Q), ALU.subtract, ALU.mult)
                V.tensor_scalar(spare_f[:], steps_f[:], float(P * Q), None, ALU.mult)
                dve.drain()
                V.tensor_tensor(rows_f[:], rows_f[:], steps_end[:], ALU.is_ge)
                V.tensor_tensor(spare_f[:], steps_end[:], spare_f[:], ALU.is_gt)
                dve.drain()
                V.tensor_tensor(steps_f[:], steps_f[:], rows_f[:], ALU.subtract)
                dve.drain()
                V.tensor_tensor(steps_f[:], steps_f[:], spare_f[:], ALU.add)
                dve.drain()
                V.tensor_tensor_scan(steps_end[:], steps_f[:], zeros_b[:], 0.0, ALU.add, ALU.add)
                dve.drain()
                V.tensor_tensor(steps_f[:], steps_end[:], steps_f[:], ALU.subtract)
                V.tensor_scalar(spare_f[:, 0:1], steps_end[:, NBK - 1:NBK], 1.0, None, ALU.add)
                dve.drain()
                V.tensor_copy(pairs_i[s][:], spare_f[:, 0:1])
                V.scalar_tensor_tensor(first_slot[s][:], steps_f[:], float(P * Q), bank[2][:, 0:NBK], ALU.mult, ALU.add)
                dve.drain()
                V.tensor_scalar(pairs_i[s][:], pairs_i[s][:], 1, None, ALU.arith_shift_right)
                V.tensor_scalar(first_slot[s][:], first_slot[s][:], float(K), None, ALU.mult)
                V.memset(block_f[:], 0.0)
                for b in range(NBK - 1):
                    dve.drain()
                    V.scalar_tensor_tensor(block_f[:], step_no[:], steps_end[:, b:b + 1], block_f[:],
                                           ALU.is_ge, ALU.add)
                dve.drain()
                V.tensor_copy(block_i[s][:], block_f[:])
                dve.drain()
                dve.sem_inc(s_first, 1)

            def chunk_rows(s, chunk, c):
                t = bass.ds(chunk * CH, CH)
                order = chunk + s * NCH
                chunk_hots(s, chunk, c)
                for n, (a, z) in enumerate(PARTS):
                    dve.wait_ge(s_keyrow, order * len(PARTS) + (n + 1))
                    for k in range(a, z):
                        ins = V.scalar_tensor_tensor(same[:, k, :], bank[2 + n % 2][:, (k - a) * P:(k - a + 1) * P],
                                                     key_c[c][:, k:k + 1], after[:], ALU.is_equal, ALU.mult,
                                                     accum_out=rank[:, k:k + 1])
                    ins.then_inc(s_ranked, 1)
                if s == 0:
                    V.tensor_copy(chunkA[c][:, :, C_NORM], norm_u[:, t])
                    V.tensor_copy(chunkA[c][:, :, C_LOCAL], local_of[0][:, t])
                    V.tensor_copy(chunkA[c][:, :, C_SRC], keyf[1][:, t])
                    V.tensor_copy(chunkA[c][:, :, C_REL], rel_u[:, t])
                else:
                    V.tensor_copy(chunkB[c][:, :, B_LOCAL], local_of[1][:, t])
                    V.tensor_copy(chunkB[c][:, :, B_DST], keyf[0][:, t])
                dve.wait_ge(s_taken, order * CH + (s + CH + 1))
                V.tensor_tensor(slot_p[:], bank[4][:, 0:CH * NBK].rearrange("p (t b) -> p t b", b=NBK),
                                in_blk[c][:], ALU.mult)
                dve.drain()
                V.tensor_reduce(slot_f[:], slot_p[:], AX_X, ALU.add)
                dve.drain()
                V.tensor_tensor(slot_f[:], slot_f[:], rank[:], ALU.add)
                dve.drain()
                V.tensor_copy(chunk_at[c][:], slot_f[:])
                dve.drain()
                dve.sem_inc(s_chunk, 1)

            dve.sem_inc(s_ranked, 2)
            for s in range(2):
                for c in range(2):
                    if s == 1:
                        dve.wait_ge(s_scat[c], NCH // 2 * 16 * CH)
                    chunk_rows(s, c, c)
                with dve.Fori(1, NCH // 2) as i:
                    for c in range(2):
                        dve.wait_ge(s_scat[c], i * (16 * CH) + s * (NCH // 2 * 16 * CH))
                        chunk_rows(s, i * 2 + c, c)

            def root(values, ready):
                values().then_inc(s_sqin, 1)
                dve.wait_ge(s_sqout, ready)

            def layer_norm(ready):
                dve.drain()
                V.tensor_reduce(nstat[0][:], x[:], AX_X, ALU.add)
                dve.drain()
                V.tensor_scalar(nstat[2][:], nstat[0][:], 1.0 / FEAT, None, ALU.mult)
                dve.drain()
                V.tensor_tensor(h[:], x[:], wide(nstat[2][:], FEAT), ALU.subtract)
                dve.drain()
                V.tensor_tensor(tmp[:], h[:], h[:], ALU.mult)
                dve.drain()
                V.tensor_reduce(nstat[2][:], tmp[:], AX_X, ALU.add)
                dve.drain()
                root(lambda: V.tensor_scalar(nstat[0][:], nstat[2][:], 1.0 / FEAT, LN_EPS, ALU.mult, ALU.add), ready)
                V.reciprocal(nstat[2][:], nstat[1][:])
                dve.drain()
                V.tensor_tensor(h[:], h[:], wide(nstat[2][:], FEAT), ALU.mult)
                dve.drain()
                V.tensor_scalar(h[:], h[:], 0.0, None, ALU.max)
                dve.drain()

            def one_hots(s, step, p):
                for q in range(Q):
                    ins = V.tensor_scalar(hot[p][:, q, :], iota_row[:], row_loc[s][:, bass.ds(step * Q + q, 1)],
                                          None, ALU.is_equal)
                return ins

            def block_at(s, step):
                return dve.value_load(block_i[s][0:1, bass.ds(step, 1)], min_val=0, max_val=NBK - 1)

            def add_pass(ps, s, pairs, done, weights=None):
                V.memset(acc1, 0.0)
                dve.drain()
                with dve.Fori(0, pairs) as i:
                    for p in range(2):
                        step = i * 2 + p
                        n = done * pairs * 2 + i * 2 + p
                        ins = one_hots(s, step, p)
                        if weights is not None:
                            dve.wait_ge(ps.landed[p], i * (16 * SLOTS) + 16 * SLOTS)
                            w = edgeA[:, bass.ds(step * SLOTS, SLOTS), weights]
                            r = rows[p][:, :, 0:FEAT]
                            V.tensor_tensor(r, r, w.unsqueeze(2).broadcast_to([P, SLOTS, FEAT]), ALU.mult)
                            dve.drain()
                            dve.sem_inc(ps.hot, 1)
                        else:
                            ins.then_inc(ps.hot, 1)
                        blk = block_at(s, step)
                        dve.wait_ge(ps.summed, n + 1)
                        a = acc1[:, bass.ds(blk * FEAT, FEAT)]
                        V.tensor_tensor(a, a, bank[p][:, 0:FEAT], ALU.add).then_inc(ps.added, 1)
                        dve.drain()

            for ps in (pass0, pass1, pass2):
                dve.sem_inc(ps.added, 2)
            for credit in (g_val, g_valA, pass3.summed):
                dve.sem_inc(credit, 1)
            dve.sem_inc(s_hT, 2)
            pairsA, pairsB = pairs_of(dve, 0), pairs_of(dve, 1)

            layer_norm(1)
            V.tensor_copy(tbl[:, :, 0:FEAT], h[:])
            dve.drain()
            dve.sem_inc(s_t0, 1)
            dve.wait_ge(s_edge, 32)
            for s, edges, column in ((0, edgeA, C_LOCAL), (1, edgeB, B_LOCAL)):
                V.tensor_copy(row_loc[s][:], edges[:].rearrange("p (g k) w -> p g k w", k=K)[:, :, 0, column])
            V.tensor_scalar(empty[:], edgeA[:, :, C_LOCAL], 0.0, FAR, ALU.is_lt, ALU.mult)
            add_pass(pass0, 0, pairsA, 0)
            V.tensor_tensor(x[:], x[:], a1, ALU.add)
            root(lambda: V.tensor_scalar(nstat[0][:], counts[0][:], 1.0, None, ALU.add), 2)
            V.reciprocal(dinv[:], nstat[1][:])

            layer_norm(3)
            with dve.Fori(0, NBK // 2) as i:
                for p in range(2):
                    dve.wait_ge(s_hT, i * 2 + (p + 1))
                    V.tensor_copy(h_blk[p][:], h[:, bass.ds(i * 2 + p, 1), :].rearrange("p a c -> p (a c)")
                                  ).then_inc(s_hblk, 1)
            add_pass(pass1, 0, pairsA, 0, C_NORM)
            V.scalar_tensor_tensor(x[:], a1, 0.0, x[:], ALU.max, ALU.add)

            layer_norm(4)
            V.tensor_copy(hh, h[:])
            with dve.Fori(0, STEPS_L2) as k:
                dve.drain()
                V.tensor_tensor(tmp[:], h[:], wide(dinv[:], FEAT), ALU.mult)
                dve.drain()
                dve.sem_inc(s_t2, 1)
                add_pass(pass2, 1, pairsB, k)
                dve.wait_ge(s_tab2, k * 16 + 16)
                V.tensor_tensor(tmp[:], tmp[:], a1, ALU.add)
                dve.drain()
                V.tensor_tensor(tmp[:], tmp[:], wide(dinv[:], FEAT), ALU.mult)
                dve.drain()
                V.tensor_tensor(tmp[:], h[:], tmp[:], ALU.subtract)
                dve.drain()
                V.scalar_tensor_tensor(tmp[:], tmp[:], -GAMMA * 2.0 * (1.0 - LAMBDA_AMP), h[:], ALU.mult, ALU.add)
                dve.drain()
                V.tensor_tensor(tmp[:], tmp[:], hh, ALU.subtract)
                dve.drain()
                V.tensor_tensor(h[:], tmp[:], tmp[:], ALU.mult)
                dve.drain()
                V.tensor_reduce(nstat[2][:], h[:], AX_X, ALU.add)
                dve.drain()
                root(lambda: V.tensor_copy(nstat[0][:], nstat[2][:]), k + 5)
                V.tensor_scalar(nstat[2][:], nstat[1][:], 1e-30, None, ALU.max)
                V.tensor_scalar(nstat[0][:], nstat[1][:], GAMMA * LAMBDA_AMP, 0.0, ALU.subtract, ALU.max)
                dve.drain()
                V.reciprocal(nstat[2][:], nstat[2][:])
                dve.drain()
                V.tensor_tensor(nstat[0][:], nstat[0][:], nstat[2][:], ALU.mult)
                dve.drain()
                V.tensor_tensor(tmp[:], tmp[:], wide(nstat[0][:], FEAT), ALU.mult)
                dve.drain()
                V.tensor_tensor(h[:], hh, tmp[:], ALU.add)
            dve.drain()
            V.tensor_tensor(x[:], x[:], h[:], ALU.add)

            layer_norm(5 + STEPS_L2)
            dve.sem_inc(s_lwfree, 1)
            with dve.Fori(0, LAYERS) as l:
                V.tensor_scalar(h[:], h[:], 0.0, None, ALU.max)
                dve.wait_ge(s_lw, l * 64 + 64)
                V.tensor_copy(att_b[:], wide(att[:], P)).then_inc(s_attb, 1)
                dve.wait_ge(s_vec, l + 1)
                V.tensor_copy(vec[:].rearrange("p c k -> p (c k)"), bank[7][:, 0:2 * HEADS * AW])
                dve.drain()
                V.tensor_copy(tbl[:, :, 0:FEAT], h[:])
                tgt_v = a_tgt[:].rearrange("p (b h) -> p b h", h=HEADS)
                tmp_v = a_tmp[:].rearrange("p (b h) -> p b h", h=HEADS)
                for c in range(2 * HEADS):
                    w = vec[:, c:c + 1, 0:FEAT].broadcast_to([P, NBK, FEAT])
                    V.tensor_tensor(tmp[:], h[:], w, ALU.mult)
                    dve.drain()
                    dest = tbl[:, :, FEAT + c] if c < HEADS else tgt_v[:, :, c - HEADS]
                    V.tensor_reduce(dest, tmp[:], AX_X, ALU.add)
                    dve.drain()
                dve.sem_inc(s_t3, 1)
                V.tensor_tensor(tmp_v, tgt_v, tbl[:, :, FEAT:FEAT + HEADS], ALU.add)
                dve.drain()
                V.tensor_tensor(tmp_v, tmp_v, vec[:, 0:HEADS, AW - 1].unsqueeze(1).broadcast_to([P, NBK, HEADS]), ALU.add)
                V.memset(acc[:], 0.0)
                dve.drain()
                V.scalar_tensor_tensor(a_max[:], a_tmp[:], 0.2, a_tmp[:], ALU.mult, ALU.max)
                av = acc[:].rearrange("p (b h c) -> p b h c", h=HEADS, c=AW)
                for hd in range(HEADS):
                    V.tensor_copy(av[:, :, hd, 0:FEAT], h[:])
                V.memset(accv[:, :, AW - 1], 1.0)
                dve.drain()

                def by_row(a):
                    return a.rearrange("p (q h) -> p q h", h=HEADS).unsqueeze(2).broadcast_to([P, Q, K, HEADS])

                def slots(a):
                    return a.rearrange("p (q k h) -> p q k h", k=K, h=HEADS)

                def attributes(step):
                    return edgeA[:, bass.ds(step * SLOTS, SLOTS), 0:EDGE_F + 1].unsqueeze(2).broadcast_to(
                        [P, SLOTS, HEADS, EDGE_F + 1])

                def targets(step, p):
                    blk = block_at(0, step)
                    V.tensor_copy(tgt_q[:], a_tgt[:, bass.ds(blk * HEADS, HEADS)])
                    one_hots(0, step, p)
                    dve.drain()
                    dve.sem_inc(pass3.hot, 1)
                    return blk

                def edge_part(step):
                    for q in range(Q):
                        V.tensor_scalar(far[:, q, :], iota_row[:], row_loc[0][:, bass.ds(step * Q + q, 1)],
                                        FAR, ALU.not_equal, ALU.mult)
                    av_e = vec[:, 0:HEADS, FEAT:AW].unsqueeze(1).broadcast_to([P, SLOTS, HEADS, EDGE_F + 1])
                    V.tensor_tensor(edge_p, attributes(step), av_e, ALU.mult)
                    dve.drain()
                    es = edge_s[:].rearrange("p (t h) -> p t h", h=HEADS)
                    V.tensor_reduce(es, edge_p, AX_X, ALU.add)
                    dve.drain()
                    V.tensor_tensor(es, es, wide(empty[:, bass.ds(step * SLOTS, SLOTS)], HEADS), ALU.add)
                    dve.drain()

                def score(number, p, turn):
                    es = edge_s[:].rearrange("p (t h) -> p t h", h=HEADS)
                    dve.wait_ge(pass3.landed[p], turn * (16 * SLOTS))
                    V.tensor_tensor(es, es, rows[p][:, :, FEAT:FEAT + HEADS], ALU.add)
                    dve.drain()
                    dve.wait_ge(g_tgte, number + 1)
                    V.tensor_tensor(slots(edge_s[:]), slots(edge_s[:]), by_row(bank[4][:, 0:Q * HEADS]), ALU.add)
                    dve.drain()
                    V.scalar_tensor_tensor(alpha[:], edge_s[:], 0.2, edge_s[:], ALU.mult, ALU.max)
                    dve.drain()
                    V.tensor_reduce(row_max[:].rearrange("p (q h) -> p q h", h=HEADS),
                                    alpha[:].rearrange("p (q k h) -> p q h k", k=K, h=HEADS), AX_X, ALU.max)
                    dve.drain()
                    for hd in range(HEADS):
                        for q in range(Q):
                            ins = V.scalar_tensor_tensor(scored[:, hd, q, :], hot[p][:, q, :],
                                                         row_max[:, q * 2 + hd:q * 2 + hd + 1], far[:, q, :],
                                                         ALU.mult, ALU.add)
                        ins.then_inc(g_scored, 1)

                def raise_max(blk, number, p):
                    for hd in range(HEADS):
                        dve.wait_ge(g_across, number * HEADS + (hd + 1))
                        V.tensor_reduce(gmax[:, hd:hd + 1], bank[2 + hd][:, 0:Q * P], AX_X, ALU.max)
                    dve.drain()
                    mx = a_max[:, bass.ds(blk * HEADS, HEADS)]
                    V.tensor_tensor(newmax[:], mx, gmax[:], ALU.max)
                    dve.drain()
                    V.tensor_tensor(drop[p][:], mx, newmax[:], ALU.subtract)
                    dve.drain()
                    dve.sem_inc(g_newmax, 1)
                    V.tensor_copy(mx, newmax[:])

                def below_max(number):
                    dve.wait_ge(g_maxe, number + 1)
                    V.tensor_tensor(slots(argx[:]), slots(alpha[:]), by_row(bank[5][:, 0:Q * HEADS]),
                                    ALU.subtract).then_inc(g_arg, 1)

                def weigh(step, p):
                    exv = ex[:].rearrange("p (t h) -> p t h", h=HEADS)
                    V.tensor_tensor(val[:, :, 0, 0:FEAT], rows[p][:, :, 0:FEAT], wide(exv[:, :, 0], FEAT), ALU.mult)
                    V.tensor_tensor(val[:, ACT_SLOTS:, 1, 0:FEAT], rows[p][:, ACT_SLOTS:, 0:FEAT],
                                    wide(exv[:, ACT_SLOTS:, 1], FEAT), ALU.mult)
                    V.tensor_tensor(val[:, :, :, FEAT:AW], attributes(step),
                                    exv.unsqueeze(3).broadcast_to([P, SLOTS, HEADS, EDGE_F + 1]), ALU.mult)
                    dve.drain()
                    dve.sem_inc(g_val, 1)

                def add(blk, n, ahead, p):
                    dve.wait_ge(g_keep, ahead)
                    dve.wait_ge(pass3.summed, n + 2)
                    for hd in range(HEADS):
                        a = acc[:, bass.ds(blk * (HEADS * AW) + hd * AW, AW)]
                        V.scalar_tensor_tensor(a, a, keep[p][:, hd:hd + 1], bank[6 + p][:, hd * AW:(hd + 1) * AW],
                                               ALU.mult, ALU.add)
                    dve.drain()

                first = l * (pairsA * 2 + 1)
                blk = targets(0, 0)
                edge_part(0)
                score(first, 0, l * (pairsA + 1) + 1)
                raise_max(blk, first, 0)
                below_max(first)
                with dve.Fori(0, pairsA) as i:
                    blk = None
                    for p in range(2):
                        step = i * 2 + p
                        n = l * pairsA * 2 + i * 2 + p
                        ahead = first + i * 2 + (p + 1)
                        turn = l * pairsA + i + 1 if p == 0 else l * (pairsA + 1) + i + 2
                        before_blk = blk
                        blk = targets(step + 1, 1 - p)
                        dve.wait_ge(g_ex, ahead)
                        weigh(step, p)
                        edge_part(step + 1)
                        score(ahead, 1 - p, turn)
                        add(block_at(0, step) if p == 0 else before_blk, n, ahead, p)
                        raise_max(blk, ahead, 1 - p)
                        below_max(ahead)
                dve.drain()

                V.tensor_scalar(a_tmp[:], accv[:, :, AW - 1], 1e-16, None, ALU.add)
                dve.drain()
                V.reciprocal(a_tmp[:], a_tmp[:])
                dve.drain()
                V.tensor_scalar(a_tmp[:], a_tmp[:], 1.0 / HEADS, None, ALU.mult)
                dve.drain()

                def mean_part(m, b, p):
                    c = FB * HEADS
                    V.tensor_tensor(agg[p], acc[:, bass.ds(b * (c * AW), c * AW)].rearrange("p (c k) -> p c k", k=AW),
                                    wide(a_tmp[:, bass.ds(b * c, c)], AW), ALU.mult).then_inc(s_fb, 1)

                def biased(m, b, p):
                    dve.wait_ge(s_fo, m + 1)
                    V.tensor_tensor(h[:, bass.ds(b * FB, FB), :], bank[2 + p][:, 0:FB * FEAT].rearrange("p (b c) -> p b c", c=FEAT),
                                    bias[:].unsqueeze(1).broadcast_to([P, FB, FEAT]), ALU.add)

                mean_part(l * NF, 0, 0)
                with dve.Fori(0, NF // 2) as b:
                    for p in range(2):
                        mean_part(l * NF + b * 2 + (p + 1), b * 2 + (p + 1), 1 - p)
                        biased(l * NF + b * 2 + p, b * 2 + p, p)
                biased(l * NF + NF - 1, NF - 1, 0)
                dve.drain()
                dve.sem_inc(s_lwfree, 1)
            dve.drain()
            V.tensor_tensor(x[:], x[:], h[:], ALU.add).then_inc(s_done, 1)


def kernel(x, src, dst, edge_attr_16, edge_type_16, edge_weight1, L1_gnn_weight, L3_gnn_weights,
           L3_gnn_biases, L3_gnn_edge_ws, L3_gnn_edge_bs, L3_gnn_atts):
    import numpy as np
    import concourse.bacc as bacc
    from concourse.bass_utils import run_bass_kernel_spmd

    nodes, edges = x.shape[0], src.shape[0]
    tiles, blocks, _ = sizes(nodes, edges)
    pad = tiles * P - edges

    def by_tile(a, fill):
        a = np.asarray(a)
        a = np.concatenate([a, np.full((pad,) + a.shape[1:], fill, a.dtype)])
        return np.ascontiguousarray(a.reshape((tiles, P) + a.shape[1:]).swapaxes(0, 1).reshape(P, -1))

    xp = np.concatenate([np.asarray(x), np.zeros((blocks * P - nodes, FEAT), np.float32)])
    xp = np.ascontiguousarray(xp.reshape(blocks, P, FEAT).swapaxes(0, 1).reshape(P, -1))
    w = np.asarray(L3_gnn_weights)
    layers = w.shape[0]
    w = w.reshape(layers, FEAT, HEADS, FEAT).transpose(0, 2, 1, 3)
    ew = np.asarray(L3_gnn_edge_ws).reshape(layers, HEADS, FEAT, EDGE_F).transpose(0, 1, 3, 2)
    eb = np.asarray(L3_gnn_edge_bs).reshape(layers, HEADS, 1, FEAT)
    wcat = np.concatenate([w, ew, eb], axis=2)
    atts = np.asarray(L3_gnn_atts).reshape(layers, HEADS, 2, FEAT)
    pad_key = (blocks - 1) * P
    arrays = {
        "x_in": xp,
        "src_in": by_tile(src, pad_key),
        "dst_in": by_tile(dst, pad_key),
        "type_in": by_tile(edge_type_16, 0),
        "norm_in": by_tile(edge_weight1, 0),
        "attr_in": by_tile(edge_attr_16, 0),
        "w1_in": np.ascontiguousarray(np.asarray(L1_gnn_weight).transpose(1, 0, 2).reshape(FEAT, -1)),
        "wcat_in": np.ascontiguousarray(wcat.transpose(0, 2, 1, 3).reshape(layers, AW, -1)),
        "wcatT_in": np.ascontiguousarray(wcat.transpose(0, 3, 1, 2).reshape(layers, FEAT, -1)),
        "att_in": np.ascontiguousarray(atts[:, :, ::-1].transpose(0, 3, 2, 1).reshape(layers, FEAT, -1)),
        "bias_in": np.ascontiguousarray(np.broadcast_to(np.asarray(L3_gnn_biases)[:, None], (layers, P, FEAT)).reshape(-1, FEAT)),
    }
    nc = bacc.Bacc("TRN2", target_bir_lowering=False, num_devices=1)
    args = {n: nc.dram_tensor(n, a.shape, mybir.dt.from_np(a.dtype), kind="ExternalInput").ap()
            for n, a in arrays.items()}
    out = nc.dram_tensor("out", (P, blocks * FEAT), F32, kind="ExternalOutput").ap()
    gnn_kernel(nc, nodes, out=out, **args)
    r = run_bass_kernel_spmd(nc, [arrays], core_ids=[0])
    got = r.results[0]["out"].reshape(P, blocks, FEAT).swapaxes(0, 1).reshape(-1, FEAT)[:nodes]
    return np.ascontiguousarray(got)
```

```python
from contextlib import ExitStack

import concourse.bass as bass
from concourse import mybir

ALU = mybir.AluOpType
ACT = mybir.ActivationFunctionType
AX_X = mybir.AxisListType.X
F32 = mybir.dt.float32
BF16 = mybir.dt.bfloat16
I32 = mybir.dt.int32
I16 = mybir.dt.int16

P = 128
K = 4
Q = 3
SLOTS = K * Q
ACT_SLOTS = SLOTS // 3
RELS = 16
STEPS_L2 = 3
HEADS = 2
FEAT = 64
EDGE_F = 16
AW = FEAT + EDGE_F + 1
LN_EPS = 1e-5
LAMBDA_AMP = 0.1
GAMMA = 1.0 / (2.0 * (1.0 - LAMBDA_AMP))
FAR = -1.0e30
C_ONE, C_NORM, C_LOCAL, C_SRC, C_REL = EDGE_F, EDGE_F + 1, EDGE_F + 2, EDGE_F + 3, EDGE_F + 4
WA = EDGE_F + 5


def sizes(nodes, edges):
    tiles = -(-edges // P)
    blocks = nodes // P + 1
    blocks += blocks % 2
    rows = (tiles * P + (K - 1) * (nodes + 1)) // K
    steps = (rows + blocks * Q * P) // (Q * P)
    steps += steps % 2 + 2
    return tiles, blocks, steps


def gnn_kernel(nc, nodes, x_in, src_in, dst_in, type_in, norm_in, attr_in, w1_in, wcat_in,
               wcatT_in, att_in, bias_in, out):
    T = src_in.shape[1]
    NBK = x_in.shape[1] // FEAT
    LAYERS = wcat_in.shape[0]
    NB = nodes // P + 1
    KEY_PAD = NB * P - 1
    _, _, STEPS = sizes(nodes, T * P)
    NG = STEPS * Q
    NT = NG * K
    NROW = NT * P
    NCOL = NB * P
    TURN = [(0, (NB + 1) // 2 * P), ((NB + 1) // 2 * P, NCOL)]
    WIDTH = TURN[0][1]
    BANKS = [[(a, min(a + 512, hi - lo)) for a in range(0, hi - lo, 512)] for lo, hi in TURN]
    assert len(BANKS[0]) <= 4 and NB % 2 == 1 and NB < NBK
    PER_BANK = 7
    CH = 13
    NCH = T // CH
    assert NCH * CH == T and NCH % 2 == 0
    COPIES = 4
    PARTS = [(a, min(a + COPIES, CH)) for a in range(0, CH, COPIES)]

    sortedA = nc.dram_tensor("sortedA", (NROW, WA), F32, kind="Internal").ap()
    table0 = nc.dram_tensor("table0", (NBK * P, FEAT), F32, kind="Internal").ap()
    table1 = nc.dram_tensor("table1", (NBK * P * RELS, FEAT), F32, kind="Internal").ap()
    table3 = nc.dram_tensor("table3", (NBK * P, FEAT + HEADS), F32, kind="Internal").ap()
    dense = nc.dram_tensor("dense", (2, NCOL, NCOL), BF16, kind="Internal").ap()

    with ExitStack() as ctx:
        def sb(name, shape, dt=F32):
            return ctx.enter_context(nc.sbuf_tensor(name, shape, dt))

        def sem(name):
            return ctx.enter_context(nc.semaphore(name))

        bank = [ctx.enter_context(nc.psum_tensor(f"bank{i}", [P, 512], F32)) for i in range(8)]

        iota_row = sb("iota_row", [P, P])
        ident = sb("ident", [P, P])
        identb = sb("identb", [P, P], BF16)
        before = sb("before", [P, P])
        after = sb("after", [P, P])
        ones = sb("ones", [P, P])
        zerosb = sb("zerosb", [P, 512], BF16)
        step_no = sb("step_no", [P, STEPS])

        edgeA = sb("edgeA", [P, NT, WA])

        early = edgeA[:].rearrange("p t w -> p (t w)")
        taken = [0]

        def early_t(dt=F32):
            lo = taken[0]
            taken[0] += T
            assert taken[0] <= NT * WA
            return early[:, lo:lo + T] if dt is F32 else early[:, lo:lo + T].bitcast(dt)

        key_i = [early_t(I32) for s in range(2)]
        type_i = early_t(I32)
        part_i = early_t(I32)
        keyf = [early_t() for s in range(2)]
        norm_u = early_t()
        rel_u = early_t()
        block_of = early_t()
        local_of = early_t()
        counts = sb("counts", [P, NBK])
        rows_i = sb("rows_i", [P, NBK], I32)
        rows_f = sb("rows_f", [P, NBK])
        steps_i = sb("steps_i", [P, NBK], I32)
        steps_f = sb("steps_f", [P, NBK])
        steps_end = sb("steps_end", [P, NBK])
        spare_f = sb("spare_f", [P, NBK])
        zeros_b = sb("zeros_b", [P, NBK])
        first_slot = sb("first_slot", [P, NBK])
        NEXT = (CH + 1) * NBK
        next_slot = [sb(f"next_slot{r}", [P, NEXT]) for r in range(2)]
        block_f = sb("block_f", [P, STEPS])
        block_i = sb("block_i", [P, STEPS], I32)
        pairs_i = sb("pairs_i", [P, 1], I32)
        first_i = sb("first_i", [P, NBK], I32)
        end_i = sb("end_i", [P, NBK], I32)
        deep = sb("deep", [P, NBK])
        parts_i = sb("parts_i", [P, 1], I32)
        key_c = [sb(f"key_c{c}", [P, CH]) for c in range(2)]
        in_blk = [sb(f"in_blk{c}", [P, CH, NBK], BF16) for c in range(2)]
        rank = sb("rank", [P, CH])
        slot_p = sb("slot_p", [P, CH, NBK])
        slot_f = sb("slot_f", [P, CH])
        chunkA = [sb(f"chunkA{c}", [P, CH, WA]) for c in range(2)]
        chunk_at = [sb(f"chunk_at{c}", [P, CH], I32) for c in range(2)]
        FILLS = STEPS // 2

        x = sb("x", [P, NBK, FEAT])
        h = sb("h", [P, NBK, FEAT])
        tmp = sb("tmp", [P, NBK, FEAT])
        dinv = sb("dinv", [P, NBK])
        nstat = [sb(f"nstat{i}", [P, NBK]) for i in range(3)]
        acc = sb("acc", [P, NBK * HEADS * AW])
        H2 = CH * P // 2
        in_loc = [acc[:, c * H2:(c + 1) * H2].bitcast(BF16).rearrange("p (t e) -> p t e", e=P) for c in range(2)]
        same = acc[:, 2 * H2:3 * H2].bitcast(BF16).rearrange("p (t e) -> p t e", e=P)
        locT = acc[:, 3 * H2:5 * H2]
        assert 5 * H2 <= NBK * HEADS * AW
        flat = tmp[:].rearrange("p b c -> p (b c)")
        fillA = flat[:, 0:2 * SLOTS * WA].rearrange("p (r w) -> p r w", w=WA)
        accv = acc[:].rearrange("p (b c) -> p b c", b=NBK * HEADS)

        gat_w = FEAT + HEADS
        rows = [sb(f"rows{p}", [P, SLOTS, gat_w]) for p in range(2)]
        at = [sb(f"at{p}", [P, SLOTS], I32) for p in range(2)]
        hot = [sb(f"hot{p}", [P, Q, P]) for p in range(2)]
        row_loc = sb("row_loc", [P, NG])
        empty = sb("empty", [P, NT])

        h_blk = [sb(f"h_blk{p}", [P, FEAT]) for p in range(2)]
        hT_blk = [sb(f"hT_blk{p}", [FEAT, P]) for p in range(2)]

        wcat = sb("wcat", [AW, HEADS * FEAT])
        wcatT = sb("wcatT", [FEAT, HEADS * AW])
        att = sb("att", [FEAT, 2 * HEADS])
        att_b = sb("att_b", [FEAT, 2 * HEADS, P])
        bias = sb("bias", [P, FEAT])
        edge_y = sb("edge_y", [P, 2 * RELS * FEAT])
        hh = edge_y[:, 0:NBK * FEAT].rearrange("p (b c) -> p b c", c=FEAT)
        scored = edge_y[:, 0:HEADS * Q * P].rearrange("p (h q e) -> p h q e", h=HEADS, q=Q)
        hotT = edge_y[:, HEADS * Q * P:(HEADS + 1) * Q * P]
        edge_p = edge_y[:, (HEADS + 1) * Q * P:(HEADS + 1) * Q * P + SLOTS * HEADS * (EDGE_F + 1)].rearrange(
            "p (t h f) -> p t h f", t=SLOTS, h=HEADS)
        vec = sb("vec", [P, 2 * HEADS, AW])
        tbl = sb("tbl", [P, NBK, gat_w])
        a_tgt = sb("a_tgt", [P, NBK * HEADS])
        a_max = sb("a_max", [P, NBK * HEADS])
        a_tmp = sb("a_tmp", [P, NBK * HEADS])
        far = sb("far", [P, Q, P])
        row_max = sb("row_max", [P, Q * HEADS])
        tgt_q = sb("tgt_q", [P, HEADS])
        edge_s = sb("edge_s", [P, SLOTS * HEADS])
        alpha = sb("alpha", [P, SLOTS * HEADS])
        argx = sb("argx", [P, SLOTS * HEADS])
        ex = sb("ex", [P, SLOTS * HEADS])
        gmax = sb("gmax", [P, HEADS])
        newmax = sb("newmax", [P, HEADS])
        drop = [sb(f"drop{p}", [P, HEADS]) for p in range(2)]
        keep = [sb(f"keep{p}", [P, HEADS]) for p in range(2)]
        hilo = sb("hilo", [P, 2, NCOL], BF16)
        VAL = SLOTS * HEADS * AW
        assert VAL <= NCOL
        val = hilo[:].rearrange("p a c -> p (a c)")[:, 0:2 * VAL].bitcast(F32).rearrange(
            "p (t h c) -> p t h c", t=SLOTS, h=HEADS)
        FB = 2
        NF = NBK // FB
        assert NF * FB == NBK and NF % 2 == 1
        AG = FB * HEADS * AW
        val_f = val.rearrange("p t h c -> p (t h c)")
        agg = [val_f[:, p * AG:(p + 1) * AG].rearrange("p (c k) -> p c k", k=AW) for p in range(2)]
        AT = FB * HEADS * P
        aggT = [val_f[0:AW, 2 * AG + p * AT:2 * AG + (p + 1) * AT].rearrange("p (c e) -> p c e", e=P)
                for p in range(2)]
        assert 2 * AG + 2 * AT <= VAL
        w1 = val[0:FEAT].rearrange("p t h c -> p (t h c)")[:, 0:RELS * FEAT]
        W2 = WIDTH // 2
        assert 4 * W2 <= NBK * HEADS * AW and 2 * W2 <= 2 * RELS * FEAT and NCOL // 2 <= NBK * FEAT
        in_src = [a[:, n * W2:(n + 1) * W2].bitcast(BF16) for a, many in ((acc, 4), (edge_y, 2)) for n in range(many)]
        NSRC = len(in_src)
        assert SLOTS % NSRC == 0 and NSRC >= K
        hotb = hot[1][:].rearrange("p q e -> p (q e)")[:, 0:Q * P // 2].bitcast(BF16).rearrange(
            "p (q e) -> p q e", e=P)
        node_no = h[:].rearrange("p b c -> p (b c)")[:, 0:NCOL // 2].bitcast(I16)
        zpart = acc[:, 0:NBK * 3 * FEAT // 2].bitcast(BF16).rearrange("p (b c) -> p b c", b=NBK)
        z_rest = tbl[:, :, 0:FEAT]
        y_blk = [edge_y[:, p * RELS * FEAT:(p + 1) * RELS * FEAT] for p in range(2)]

        s_in = sem("s_in")
        s_w1 = sem("s_w1")
        s_fill = sem("s_fill")
        s_attr = [sem(f"s_attr{c}") for c in range(2)]
        s_scat = [sem(f"s_scat{c}") for c in range(2)]
        s_edge = sem("s_edge")
        s_tab0 = sem("s_tab0")
        s_dst = sem("s_dst")
        s_dload = [sem(f"s_dload{p}") for p in range(2)]
        s_tab3 = sem("s_tab3")
        s_lw = sem("s_lw")
        s_out = sem("s_out")
        s_aside = sem("s_aside")
        s_aside_pe = sem("s_aside_pe")
        s_aside_sp = sem("s_aside_sp")
        s_pool_c = sem("s_pool_c")
        s_const = sem("s_const")
        s_fillready = sem("s_fillready")
        s_onehot = sem("s_onehot")
        s_hist = sem("s_hist")
        s_rows = sem("s_rows")
        s_prefix = sem("s_prefix")
        s_first = sem("s_first")
        s_locT = sem("s_locT")
        s_locTc = sem("s_locTc")
        s_keyrow = sem("s_keyrow")
        s_ranked = sem("s_ranked")
        s_taken = sem("s_taken")
        s_found = sem("s_found")
        s_next = sem("s_next")
        s_chunk = sem("s_chunk")
        s_sqin = sem("s_sqin")
        s_sqout = sem("s_sqout")
        s_t0 = sem("s_t0")
        s_node_no = sem("s_node_no")
        s_hotb, s_src, s_dsum, s_hi, s_lo = ([sem(f"{name}{turn}") for turn in range(2)]
                                             for name in ("s_hotb", "s_src", "s_dsum", "s_hi", "s_lo"))
        s_z = sem("s_z")
        s_dused = sem("s_dused")
        s_t3 = sem("s_t3")
        s_hblk = sem("s_hblk")
        s_hT = sem("s_hT")
        s_hTc = sem("s_hTc")
        s_y = sem("s_y")
        s_yc = sem("s_yc")
        s_yfree = sem("s_yfree")
        s_tab1 = [sem(f"s_tab1{p}") for p in range(2)]
        s_attb = sem("s_attb")
        s_vec = sem("s_vec")
        s_lwfree = sem("s_lwfree")
        s_fb = sem("s_fb")
        s_fT = sem("s_fT")
        s_fTc = sem("s_fTc")
        s_fo = sem("s_fo")
        s_fread = sem("s_fread")
        s_done = sem("s_done")

        class Pass:
            def __init__(self, name, buffers):
                self.idx = sem(f"{name}_idx")
                self.landed = [sem(f"{name}_landed{p}") for p in range(buffers)]
                self.hot = sem(f"{name}_hot")
                self.summed = sem(f"{name}_summed")
                self.added = sem(f"{name}_added")

        pass0, pass1, pass3 = Pass("sum", Q), Pass("rel", Q), Pass("gat", 2)
        g_T = sem("g_T")
        g_Tc = sem("g_Tc")
        g_tgte = sem("g_tgte")
        g_scored = sem("g_scored")
        g_across = sem("g_across")
        g_newmax = sem("g_newmax")
        g_keep = sem("g_keep")
        g_maxe = sem("g_maxe")
        g_arg = sem("g_arg")
        g_ex = sem("g_ex")
        g_val = sem("g_val")
        g_valA = sem("g_valA")

        def pairs_of(eng):
            return eng.value_load(pairs_i[0:1, 0:1], min_val=1, max_val=STEPS // 2 - 1)

        def parts_of(eng):
            return eng.value_load(parts_i[0:1, 0:1], min_val=1, max_val=2)

        def of_block(eng, a, b, low):
            return eng.value_load(a[0:1, bass.ds(b, 1)], min_val=low, max_val=STEPS)

        block = ctx.enter_context(nc.Block())

        @block.sync
        def _(sp):
            sp.dma_start(key_i[0][:], dst_in).then_inc(s_in, 16)
            sp.dma_start(key_i[1][:], src_in).then_inc(s_in, 16)
            sp.dma_start(type_i[:], type_in).then_inc(s_in, 16)
            sp.dma_start(norm_u[:], norm_in).then_inc(s_in, 16)
            sp.dma_start(x[:].rearrange("p b c -> p (b c)"), x_in).then_inc(s_in, 16)
            sp.wait_ge(s_fillready, 1)
            va = sortedA.rearrange("(p k r) w -> k p (r w)", p=P, k=FILLS)
            for k in range(FILLS):
                sp.dma_start(va[k], flat[:, 0:2 * SLOTS * WA]).then_inc(s_fill, 16)
            def load_attr(chunk, c):
                sp.dma_start(chunkA[c][:, :, 0:EDGE_F],
                             attr_in[:, bass.ds(chunk * (CH * EDGE_F), CH * EDGE_F)]
                             .rearrange("p (t f) -> p t f", f=EDGE_F)).then_inc(s_attr[c], 16)

            for c in range(2):
                load_attr(c, c)
            with sp.Fori(1, NCH // 2) as i:
                for c in range(2):
                    sp.wait_ge(s_scat[c], i * (16 * CH))
                    load_attr(i * 2 + c, c)
            for c in range(2):
                sp.wait_ge(s_scat[c], NCH // 2 * 16 * CH)
            sp.dma_start(edgeA[:].rearrange("p (g j) w -> p g (j w)", j=K),
                         sortedA.rearrange("(g p j) w -> p g (j w)", p=P, j=K)).then_inc(s_edge, 16)
            sp.wait_ge(s_t0, 1)
            sp.dma_start(table0.rearrange("(b p) c -> p b c", p=P),
                         tbl[:, :, 0:FEAT]).then_inc(s_tab0, 16)
            def store_dense(turn):
                lo, hi = TURN[turn]
                with sp.Fori(0, NB) as b:
                    sp.wait_ge(s_lo[turn], b * len(BANKS[turn]) + 2 * len(BANKS[turn]))
                    sp.dma_start(dense[:, bass.ds(b * P, P), lo:hi].rearrange("a p c -> p a c"),
                                 hilo[:, :, 0:hi - lo]).then_inc(s_dst, 16)

            sp.sem_inc(s_dst, 16)
            store_dense(0)
            sp.wait_ge(s_dst, NB * 16 + 16)
            sp.dma_start(w1, w1_in).then_inc(s_w1, 16)
            t1 = table1.rearrange("(n r) c -> n (r c)", r=RELS)
            sp.sem_inc(s_yfree, 2)
            with sp.Fori(0, NBK // 2) as i:
                for p in range(2):
                    sp.wait_ge(s_yc, i * 2 + (p + 1))
                    sp.dma_start(t1[bass.ds((i * 2 + p) * P, P), :], y_blk[p]).then_inc(s_tab1[p], 16)
                    sp.wait_ge(s_tab1[p], i * 16 + 16)
                    sp.sem_inc(s_yfree, 1)
            store_dense(1)
            sp.wait_ge(s_dst, 2 * NB * 16 + 16)
            parts = parts_of(sp)

            def load_dense(part, b, p):
                sp.dma_start(hilo[:, p, :], dense[bass.ds(part, 1), bass.ds(b * P, P), :].rearrange("a p c -> (a p) c")
                             ).then_inc(s_dload[p], 16)

            sp.sem_inc(s_dused, 2)
            with sp.Fori(0, STEPS_L2) as k:
                with sp.Fori(0, parts) as part:
                    n = (k * parts + part) * NB
                    with sp.Fori(0, NB // 2) as i:
                        for p in range(2):
                            sp.wait_ge(s_dused, n + i * 2 + (p + 1))
                            load_dense(part, i * 2 + p, p)
                    sp.wait_ge(s_dused, n + NB)
                    load_dense(part, NB - 1, 0)
                    sp.wait_ge(s_dused, n + (NB + 2))
                    sp.sem_inc(s_aside_sp, 1)
            with sp.Fori(0, LAYERS) as l:
                sp.wait_ge(s_lwfree, l + 1)
                for dst, src in ((wcat, wcat_in), (wcatT, wcatT_in), (att, att_in)):
                    sp.dma_start(dst[:], src[bass.ds(l, 1), :, :].rearrange("a k n -> (a k) n")).then_inc(s_lw, 16)
                sp.dma_start(bias[:], bias_in[bass.ds(l * P, P), :]).then_inc(s_lw, 16)
                sp.wait_ge(s_t3, l + 1)
                sp.dma_start(table3.rearrange("(b p) c -> p b c", p=P), tbl[:]).then_inc(s_tab3, 16)
            sp.wait_ge(s_done, 1)
            sp.dma_start(out, x[:].rearrange("p b c -> p (b c)")).then_inc(s_out, 16)
            sp.wait_ge(s_out, 16)

        @block.gpsimd
        def _(pool):
            nc.gpsimd.iota(iota_row[:], [[1, P]], base=0, channel_multiplier=0,
                           allow_small_or_imprecise_dtypes=True).then_inc(s_pool_c, 1)
            nc.gpsimd.iota(step_no[:], [[1, STEPS]], base=0, channel_multiplier=0,
                           allow_small_or_imprecise_dtypes=True).then_inc(s_pool_c, 1)
            nc.gpsimd.memset(ident[:], 0.0).then_inc(s_pool_c, 1)
            nc.gpsimd.memset(before[:], 1.0).then_inc(s_pool_c, 1)
            nc.gpsimd.memset(after[:], 1.0).then_inc(s_pool_c, 1)
            nc.gpsimd.memset(ones[:], 1.0).then_inc(s_pool_c, 1)
            pool.wait_ge(s_pool_c, 6)
            nc.gpsimd.affine_select(out=ident[:], in_=ident[:], compare_op=ALU.not_equal, fill=1.0,
                                    base=0, pattern=[[-1, P]], channel_multiplier=1).then_inc(s_const, 1)
            nc.gpsimd.affine_select(out=before[:], in_=before[:], compare_op=ALU.is_gt, fill=0.0,
                                    base=0, pattern=[[1, P]], channel_multiplier=-1).then_inc(s_const, 1)
            nc.gpsimd.affine_select(out=after[:], in_=after[:], compare_op=ALU.is_gt, fill=0.0,
                                    base=0, pattern=[[-1, P]], channel_multiplier=1).then_inc(s_const, 1)

            pool.wait_ge(s_fill, 16 * FILLS)
            def scatter(table, chunk, c, turn):
                for t in range(CH):
                    nc.gpsimd.indirect_dma_start(
                        table, bass.IndirectOffsetOnAxis(ap=chunk_at[c][:, t:t + 1], axis=0),
                        chunk[c][:, t, :], None).then_inc(s_scat[c], 16)

            with pool.Fori(0, NCH // 2) as i:
                for c in range(2):
                    pool.wait_ge(s_chunk, i * 2 + (c + 1))
                    pool.wait_ge(s_attr[c], i * 16 + 16)
                    pool.sem_inc(s_aside, 1)
                    scatter(sortedA, chunkA, c, i)

            def gather(ps, table, width, number, p):
                pool.wait_ge(ps.idx, number + 1)
                pool.sem_inc(s_aside, 1)
                for t in range(SLOTS):
                    nc.gpsimd.indirect_dma_start(
                        rows[p][:, t, 0:width], None, table,
                        bass.IndirectOffsetOnAxis(ap=at[p][:, t:t + 1], axis=0)
                        ).then_inc(ps.landed[p], 16)

            def gathers(ps, table, column):
                with pool.Fori(0, steps0) as n:
                    for q in range(Q):
                        pool.wait_ge(ps.summed, n * Q + (q + 1))
                        nc.gpsimd.tensor_copy(at[0][:, q * K:(q + 1) * K],
                                              edgeA[:, bass.ds(n * SLOTS + q * K, K), column]).then_inc(ps.idx, 1)
                        pool.wait_ge(ps.idx, n * Q + (q + 1))
                        pool.sem_inc(s_aside, 1)
                        for t in range(q * K, (q + 1) * K):
                            nc.gpsimd.indirect_dma_start(
                                rows[0][:, t, 0:FEAT], None, table,
                                bass.IndirectOffsetOnAxis(ap=at[0][:, t:t + 1], axis=0)
                                ).then_inc(ps.landed[q], 16)

            pool.wait_ge(s_t0, 1)
            nc.gpsimd.iota(node_no, [[1, NCOL]], base=0, channel_multiplier=0).then_inc(s_node_no, 1)
            pool.wait_ge(s_edge, 16)
            pairsA = pairs_of(pool)
            steps0 = of_block(pool, end_i, NB - 1, 1)
            pool.wait_ge(s_tab0, 16)
            pool.sem_inc(s_aside, 1)
            gathers(pass0, table0, C_SRC)
            pool.wait_ge(s_hblk, NBK)
            nc.gpsimd.iota(node_no, [[1, NCOL]], base=0, channel_multiplier=0).then_inc(s_node_no, 1)
            for p in range(2):
                pool.wait_ge(s_tab1[p], 16 * (NBK // 2))
            pool.sem_inc(s_aside, 1)
            gathers(pass1, table1, C_REL)
            with pool.Fori(0, LAYERS) as l:
                pool.wait_ge(s_tab3, l * 16 + 16)
                pool.sem_inc(s_aside, 1)
                gather(pass3, table3, gat_w, l * (pairsA * 2 + 2), 0)
                with pool.Fori(0, pairsA) as i:
                    for p in range(2):
                        n = l * pairsA * 2 + i * 2 + p
                        pool.wait_ge(g_val, n + 1)
                        pool.wait_ge(g_valA, n + 1)
                        gather(pass3, table3, gat_w, l * (pairsA * 2 + 2) + i * 2 + (p + 1), 1 - p)

        @block.tensor
        def _(pe):
            pe.wait_ge(s_const, 4)
            pe.wait_ge(s_fillready, 1)
            nc.tensor.matmul(bank[0][:, 0:NBK], ident[:], zeros_b[:], start=True, stop=False, skip_group_check=True)
            with pe.Fori(0, NCH // 2) as i:
                for c in range(2):
                    pe.wait_ge(s_onehot, i * 2 + (c + 1))
                    for t in range(CH):
                        mm = nc.tensor.matmul(bank[0][:, 0:NBK], in_loc[c][:, t, :], in_blk[c][:, t, :],
                                              start=False, stop=False, skip_group_check=True)
                    mm.then_inc(s_hist, 1)
            pe.wait_ge(s_rows, 1)
            nc.tensor.matmul(bank[2][:, 0:NBK], before[:], rows_f[:], start=True, stop=True)
            nc.tensor.matmul(bank[4][:, 0:NBK], ones[:], deep[:], start=True, stop=True)
            nc.tensor.matmul(bank[3][:, 0:NBK], ones[:], rows_f[:], start=True, stop=True).then_inc(s_prefix, 1)
            pe.wait_ge(s_first, 1)
            with pe.Fori(0, NCH // 2) as i:
                for c in range(2):
                    chunk = i * 2 + c
                    pe.wait_ge(s_onehot, chunk + (NCH + 1))
                    pe.wait_ge(s_next, chunk + 1)
                    taken_v = bank[5][:, 0:NEXT].rearrange("p (t b) -> p t b", b=NBK)
                    nc.tensor.matmul(taken_v, ident[:],
                                     next_slot[1 - c][:, CH * NBK:NEXT].unsqueeze(1).broadcast_to([P, CH + 1, NBK]),
                                     start=True, stop=False, skip_group_check=True)
                    for t in range(CH):
                        mm = nc.tensor.matmul(taken_v[:, t + 1:CH + 1, :], in_loc[c][:, t, :],
                                              in_blk[c][:, t:t + 1, :].broadcast_to([P, CH - t, NBK]),
                                              start=False, stop=False, skip_group_check=True)
                    mm.then_inc(s_taken, 1)
                    for n, (a, z) in enumerate(PARTS):
                        part = chunk * len(PARTS) + n
                        pe.wait_ge(s_locTc, part + 1)
                        for t in range(a, z):
                            mm = nc.tensor.matmul(bank[n % 2][:, (t - a) * P:(t - a + 1) * P],
                                                  in_loc[c][:, t, :], identb[:], start=True, stop=True)
                        mm.then_inc(s_locT, 1)
                        pe.wait_ge(s_ranked, part + 1)
                        for t in range(a, z):
                            mm = nc.tensor.matmul(bank[2 + n % 2][:, (t - a) * P:(t - a + 1) * P],
                                                  key_c[c][:, t:t + 1].broadcast_to([P, P]), ident[:],
                                                  start=True, stop=True)
                        mm.then_inc(s_keyrow, 1)
                    pe.wait_ge(s_next, chunk + 2)
                    for t in range(CH):
                        if t % COPIES == 0:
                            pe.wait_ge(s_locTc, chunk * len(PARTS) + (t // COPIES + 3))
                        mm = nc.tensor.matmul(bank[4 + 2 * c][:, t * NBK:(t + 1) * NBK], locT[:, t * P:(t + 1) * P],
                                              next_slot[c][:, t * NBK:(t + 1) * NBK], start=True, stop=True)
                    mm.then_inc(s_found, 1)

            pairsA, parts = pairs_of(pe), parts_of(pe)

            def dense_turn(turn, ps):
                banks = BANKS[turn]
                with pe.Fori(0, NB) as b:
                    first = of_block(pe, first_i, b, 0)
                    end = of_block(pe, end_i, b, 1)
                    pe.wait_ge(ps.added, b + 1)
                    nc.tensor.matmul(bank[7][:, 0:P], identb[:], zerosb[:, 0:P], start=True, stop=False,
                                     skip_group_check=True)
                    for n, (lo, hi) in enumerate(banks):
                        pe.wait_ge(s_lo[turn], b * len(banks) + (n + 1))
                        nc.tensor.matmul(bank[n][:, 0:hi - lo], identb[:], zerosb[:, 0:hi - lo], start=True,
                                         stop=False, skip_group_check=True)
                    with pe.Fori(first, end) as step:
                        for q in range(Q):
                            pe.wait_ge(s_hotb[turn], step * Q + (q + 1))
                            for j in range(q * K, (q + 1) * K):
                                pe.wait_ge(s_src[turn], step * SLOTS + (j + 1))
                                for n, (lo, hi) in enumerate(banks):
                                    mm = nc.tensor.matmul(bank[n][:, 0:hi - lo], hotb[:, q, :],
                                                          in_src[j % NSRC][:, lo:hi], start=False, stop=False,
                                                          skip_group_check=True)
                                mm.then_inc(s_dsum[turn], 1)
                            pe.wait_ge(ps.landed[q], step * (16 * K) + 16 * K)
                            pe.wait_ge(ps.hot, step * Q + (q + 1))
                            pe.sem_inc(s_aside_pe, 1)
                            for t in range(q * K, (q + 1) * K):
                                mm = nc.tensor.matmul(bank[7][:, 0:FEAT], hot[0][:, q, :], rows[0][:, t, 0:FEAT],
                                                      start=False, stop=False, skip_group_check=True)
                            mm.then_inc(ps.summed, 1)

            pe.wait_ge(s_node_no, 2)
            dense_turn(0, pass0)
            pe.wait_ge(s_w1, 16)
            with pe.Fori(0, NBK // 2) as i:
                for p in range(2):
                    b = i * 2 + p
                    pe.wait_ge(s_hblk, b + 1)
                    pe.sem_inc(s_aside_pe, 1)
                    nc.tensor.transpose(bank[p][0:FEAT, 0:P], h_blk[p][:], ident[:]).then_inc(s_hT, 1)
                    pe.wait_ge(s_hTc, b + 1)
                    for half in range(2):
                        nc.tensor.matmul(bank[2 + 2 * p + half][:, :], hT_blk[p][:], w1[:, half * 512:(half + 1) * 512],
                                         start=True, stop=True).then_inc(s_y, 1)
            pe.wait_ge(s_yc, NBK)
            dense_turn(1, pass1)
            def products(b, landed, p):
                pe.wait_ge(s_dload[p], landed)
                pe.sem_inc(s_aside_pe, 1)
                for c in range(NB):
                    for part in range(3):
                        mm = nc.tensor.matmul(
                            bank[c // PER_BANK][:, (c % PER_BANK) * FEAT:(c % PER_BANK + 1) * FEAT],
                            hilo[:, p, c * P:(c + 1) * P],
                            zpart[:, bass.ds(b, 1), part * FEAT:(part + 1) * FEAT].rearrange("p a c -> p (a c)"),
                            start=False, stop=False, skip_group_check=True)
                mm.then_inc(s_dused, 1)

            with pe.Fori(0, STEPS_L2) as k:
                pe.wait_ge(s_z, k + 1)
                for n in range(-(-NB // PER_BANK)):
                    nc.tensor.matmul(bank[n][:, :], identb[:], zerosb[:], start=True, stop=False,
                                     skip_group_check=True)
                with pe.Fori(0, parts) as part:
                    r = k * parts + part
                    with pe.Fori(0, NB // 2) as i:
                        for p in range(2):
                            products(i * 2 + p, (r * (NB // 2 + 1 - p) + i + 1) * 16, p)
                    products(NB - 1, (r * (NB // 2 + 1) + (NB // 2 + 1)) * 16, 0)

            def targets(number, p):
                pe.wait_ge(pass3.hot, number + 1)
                for q in range(Q):
                    tr = nc.tensor.transpose(bank[0][:, q * P:(q + 1) * P], hot[p][:, q, :], ident[:])
                tr.then_inc(g_T, 1)
                pe.wait_ge(g_Tc, number + 1)
                for q in range(Q):
                    mm = nc.tensor.matmul(bank[4][:, q * 2:q * 2 + 2], hotT[:, q * P:(q + 1) * P],
                                          tgt_q[:], start=True, stop=True)
                mm.then_inc(g_tgte, 1)

            def across(number):
                for hd in range(HEADS):
                    pe.wait_ge(g_scored, number * HEADS + (hd + 1))
                    for q in range(Q):
                        dst = bank[2 + hd][:, q * P:(q + 1) * P]
                        mm = nc.tensor.transpose(dst, scored[:, hd, q, :], ident[:])
                    mm.then_inc(g_across, 1)

            def maxima(number):
                pe.wait_ge(g_newmax, number + 1)
                for q in range(Q):
                    mm = nc.tensor.matmul(bank[5][:, q * 2:q * 2 + 2], hotT[:, q * P:(q + 1) * P],
                                          newmax[:], start=True, stop=True)
                mm.then_inc(g_maxe, 1)

            with pe.Fori(0, LAYERS) as l:
                pe.wait_ge(s_lw, l * 64 + 64)
                pe.wait_ge(s_attb, l + 1)
                for c in range(2 * HEADS):
                    hd = c % HEADS
                    mm = nc.tensor.matmul(bank[7][:, c * AW:(c + 1) * AW], att_b[:, c, :],
                                          wcatT[:, hd * AW:(hd + 1) * AW], start=True, stop=True)
                mm.then_inc(s_vec, 1)
                targets(l * (pairsA * 2 + 1), 0)
                across(l * (pairsA * 2 + 1))
                maxima(l * (pairsA * 2 + 1))
                with pe.Fori(0, pairsA) as i:
                    for p in range(2):
                        n = l * pairsA * 2 + i * 2 + p
                        ahead = l * (pairsA * 2 + 1) + i * 2 + (p + 1)
                        targets(ahead, 1 - p)
                        pe.wait_ge(g_val, n + 2)
                        pe.wait_ge(g_valA, n + 2)
                        for q in range(Q):
                            for j in range(K):
                                mm = nc.tensor.matmul(bank[6 + p][:, 0:HEADS * AW], hot[p][:, q, :],
                                                      val[:, q * K + j, :, :].rearrange("p h c -> p (h c)"),
                                                      start=(q + j == 0), stop=(q == Q - 1 and j == K - 1))
                        mm.then_inc(pass3.summed, 1)
                        across(ahead)
                        maxima(ahead)

                def transposes(m, p):
                    pe.wait_ge(s_fb, m + 1)
                    for c in range(FB * HEADS):
                        tr = nc.tensor.transpose(bank[p][0:AW, c * P:(c + 1) * P], agg[p][:, c, :], ident[:])
                    tr.then_inc(s_fT, 1)

                def through(m, p):
                    pe.wait_ge(s_fTc, m + 1)
                    pe.wait_ge(s_fread, m + 1)
                    pe.sem_inc(s_aside_pe, 1)
                    for c in range(FB):
                        for hd in range(HEADS):
                            mm = nc.tensor.matmul(bank[2 + p][:, c * FEAT:(c + 1) * FEAT],
                                                  aggT[p][:, c * HEADS + hd, :], wcat[:, hd * FEAT:(hd + 1) * FEAT],
                                                  start=(hd == 0), stop=(hd == HEADS - 1))
                    mm.then_inc(s_fo, 1)

                transposes(l * NF, 0)
                with pe.Fori(0, NF // 2) as b:
                    for p in range(2):
                        transposes(l * NF + b * 2 + (p + 1), 1 - p)
                        through(l * NF + b * 2 + p, p)
                through(l * NF + NF - 1, 0)

        @block.scalar
        def _(act):
            act.sem_inc(s_locTc, 2)
            act.wait_ge(s_first, 1)
            nc.scalar.copy(next_slot[1][:, CH * NBK:NEXT], first_slot[:]).then_inc(s_next, 1)
            with act.Fori(0, NCH // 2) as i:
                for c in range(2):
                    chunk = i * 2 + c
                    act.wait_ge(s_taken, chunk + 1)
                    nc.scalar.copy(next_slot[c][:], bank[5][:, 0:NEXT]).then_inc(s_next, 1)
                    for n, (a, z) in enumerate(PARTS):
                        act.wait_ge(s_locT, chunk * len(PARTS) + (n + 1))
                        nc.scalar.copy(locT[:, a * P:z * P], bank[n % 2][:, 0:(z - a) * P]).then_inc(s_locTc, 1)

            def roots(ready):
                act.wait_ge(s_sqin, ready)
                nc.scalar.activation(nstat[1][:], nstat[0][:], ACT.Sqrt).then_inc(s_sqout, 1)
            roots(1)

            def high_parts(turn):
                with act.Fori(0, NB) as b:
                    end = of_block(act, end_i, b, 1)
                    act.wait_ge(s_dst, b * 16 + (turn * NB * 16 + 16))
                    act.wait_ge(s_dsum[turn], end * SLOTS + SLOTS)
                    for n, (lo, hi) in enumerate(BANKS[turn]):
                        nc.scalar.copy(hilo[:, 0, lo:hi], bank[n][:, 0:hi - lo]).then_inc(s_hi[turn], 1)

            high_parts(0)
            roots(2)
            roots(3)
            with act.Fori(0, NBK // 2) as i:
                for p in range(2):
                    b = i * 2 + p
                    act.wait_ge(s_hT, b + 3)
                    nc.scalar.copy(hT_blk[p][:], bank[p][0:FEAT, 0:P]).then_inc(s_hTc, 1)
                    act.wait_ge(s_y, b * 2 + 2)
                    act.wait_ge(s_yfree, b + 1)
                    for half in range(2):
                        cp = nc.scalar.copy(y_blk[p][:, half * 512:(half + 1) * 512], bank[2 + 2 * p + half][:, :])
                    cp.then_inc(s_yc, 1)
            high_parts(1)
            roots(4)
            with act.Fori(0, STEPS_L2) as k:
                roots(k + 5)
            roots(5 + STEPS_L2)

            pairsA = pairs_of(act)

            def transposed(number):
                act.wait_ge(g_T, number + 1)
                nc.scalar.copy(hotT, bank[0][:, 0:Q * P]).then_inc(g_Tc, 1)

            def exponentials(number, p):
                act.wait_ge(g_newmax, number + 1)
                nc.scalar.activation(keep[p][:], drop[p][:], ACT.Exp).then_inc(g_keep, 1)
                act.wait_ge(g_arg, number + 1)
                nc.scalar.activation(ex[:], argx[:], ACT.Exp).then_inc(g_ex, 1)

            def indices(step, p):
                nc.scalar.copy(at[p][:], edgeA[:, bass.ds(step * SLOTS, SLOTS), C_SRC]).then_inc(pass3.idx, 1)

            with act.Fori(0, LAYERS) as l:
                for p in range(2):
                    indices(p, p)
                transposed(l * (pairsA * 2 + 1))
                exponentials(l * (pairsA * 2 + 1), 0)
                with act.Fori(0, pairsA) as i:
                    for p in range(2):
                        n = l * pairsA * 2 + i * 2 + p
                        ahead = l * (pairsA * 2 + 1) + i * 2 + (p + 1)
                        transposed(ahead)
                        act.wait_ge(g_ex, ahead)
                        act.wait_ge(pass3.summed, n + 1)
                        for t in range(ACT_SLOTS):
                            ins = nc.scalar.activation(val[:, t, 1, 0:FEAT], rows[p][:, t, 0:FEAT], ACT.Copy,
                                                       scale=ex[:, t * HEADS + 1:t * HEADS + 2])
                        ins.then_inc(g_valA, 1)
                        indices(i * 2 + (p + 2), p)
                        exponentials(ahead, 1 - p)

                def transposed_agg(m, p):
                    act.wait_ge(s_fT, m + 1)
                    nc.scalar.copy(aggT[p].rearrange("p c e -> p (c e)"), bank[p][0:AW, :]).then_inc(s_fTc, 1)

                transposed_agg(l * NF, 0)
                with act.Fori(0, NF // 2) as b:
                    for p in range(2):
                        transposed_agg(l * NF + b * 2 + (p + 1), 1 - p)

        @block.vector
        def _(dve):
            V = nc.vector

            def wide(a, n):
                return a.unsqueeze(2).broadcast_to(list(a.shape) + [n])

            dve.wait_ge(s_const, 3)
            V.tensor_copy(identb[:], ident[:]).then_inc(s_const, 1)
            V.memset(flat[:, 0:2 * SLOTS * WA], 0.0)
            V.memset(zeros_b[:], 0.0)
            V.memset(zerosb[:], 0.0)
            dve.drain()
            V.memset(fillA[:, :, C_LOCAL], -1.0)
            V.memset(fillA[:, :, C_SRC], float(KEY_PAD))
            V.memset(fillA[:, :, C_REL], float(KEY_PAD * RELS))
            dve.drain()
            dve.sem_inc(s_fillready, 1)
            for c in range(2):
                V.memset(chunkA[c][:, :, C_ONE], 1.0)
            dve.wait_ge(s_in, 80)
            for s in range(2):
                V.tensor_copy(keyf[s][:], key_i[s][:])
            V.tensor_copy(rel_u[:], type_i[:])
            dve.drain()
            V.scalar_tensor_tensor(rel_u[:], keyf[1][:], float(RELS), rel_u[:], ALU.mult, ALU.add)
            V.tensor_scalar(part_i[:], key_i[0][:], 7, None, ALU.arith_shift_right)
            dve.drain()
            V.tensor_copy(block_of[:], part_i[:])
            dve.drain()
            V.scalar_tensor_tensor(local_of[:], block_of[:], -float(P), keyf[0][:], ALU.mult, ALU.add)
            dve.drain()

            def chunk_hots(chunk, c):
                t = bass.ds(chunk * CH, CH)
                V.tensor_copy(key_c[c][:], keyf[0][:, t])
                V.tensor_tensor(in_loc[c], iota_row[:].unsqueeze(1).broadcast_to([P, CH, P]),
                                wide(local_of[:, t], P), ALU.is_equal)
                V.tensor_tensor(in_blk[c][:], iota_row[:, 0:NBK].unsqueeze(1).broadcast_to([P, CH, NBK]),
                                wide(block_of[:, t], NBK), ALU.is_equal)
                dve.drain()
                dve.sem_inc(s_onehot, 1)

            for c in range(2):
                chunk_hots(c, c)
            with dve.Fori(1, NCH // 2) as i:
                for c in range(2):
                    dve.wait_ge(s_hist, i * 2 + (c - 1))
                    chunk_hots(i * 2 + c, c)
            dve.wait_ge(s_hist, NCH)
            V.tensor_copy(counts[:], bank[0][:, 0:NBK])
            dve.drain()
            V.tensor_scalar(deep[:], counts[:], 256.0, None, ALU.is_gt)
            V.tensor_copy(rows_i[:], counts[:])
            dve.drain()
            V.tensor_scalar(rows_f[:], counts[:], float(K - 1), None, ALU.add)
            dve.drain()
            V.tensor_copy(rows_i[:], rows_f[:])
            dve.drain()
            V.tensor_scalar(rows_i[:], rows_i[:], K.bit_length() - 1, None, ALU.arith_shift_right)
            dve.drain()
            V.tensor_copy(rows_f[:], rows_i[:])
            dve.drain()
            dve.sem_inc(s_rows, 1)
            dve.wait_ge(s_prefix, 1)
            V.tensor_scalar(steps_f[:], bank[3][:, 0:NBK], float(P * Q - 1), 1.0 / (P * Q), ALU.add, ALU.mult)
            V.tensor_scalar(steps_end[:], bank[3][:, 0:NBK], 1.0, None, ALU.mult)
            dve.drain()
            V.tensor_copy(steps_i[:], steps_f[:])
            dve.drain()
            V.tensor_copy(steps_f[:], steps_i[:])
            dve.drain()
            V.tensor_scalar(rows_f[:], steps_f[:], 1.0, float(P * Q), ALU.subtract, ALU.mult)
            V.tensor_scalar(spare_f[:], steps_f[:], float(P * Q), None, ALU.mult)
            dve.drain()
            V.tensor_tensor(rows_f[:], rows_f[:], steps_end[:], ALU.is_ge)
            V.tensor_tensor(spare_f[:], steps_end[:], spare_f[:], ALU.is_gt)
            dve.drain()
            V.tensor_tensor(steps_f[:], steps_f[:], rows_f[:], ALU.subtract)
            dve.drain()
            V.tensor_tensor(steps_f[:], steps_f[:], spare_f[:], ALU.add)
            dve.drain()
            V.tensor_scalar(steps_f[:, 0:NB], steps_f[:, 0:NB], 1.0, None, ALU.max)
            dve.drain()
            V.tensor_reduce(nstat[0][:, 0:1], bank[4][:, 0:NBK], AX_X, ALU.add)
            V.tensor_tensor_scan(steps_end[:], steps_f[:], zeros_b[:], 0.0, ALU.add, ALU.add)
            dve.drain()
            V.tensor_tensor(steps_f[:], steps_end[:], steps_f[:], ALU.subtract)
            V.tensor_scalar(spare_f[:, 0:1], steps_end[:, NBK - 1:NBK], 1.0, None, ALU.add)
            dve.drain()
            V.tensor_copy(pairs_i[:], spare_f[:, 0:1])
            V.tensor_copy(first_i[:], steps_f[:])
            V.tensor_copy(end_i[:], steps_end[:])
            V.tensor_scalar(nstat[0][:, 0:1], nstat[0][:, 0:1], 1.0, 1.0, ALU.min, ALU.add)
            V.scalar_tensor_tensor(first_slot[:], steps_f[:], float(P * Q), bank[2][:, 0:NBK], ALU.mult, ALU.add)
            dve.drain()
            V.tensor_copy(parts_i[:], nstat[0][:, 0:1])
            V.tensor_scalar(pairs_i[:], pairs_i[:], 1, None, ALU.arith_shift_right)
            V.tensor_scalar(first_slot[:], first_slot[:], float(K), None, ALU.mult)
            V.memset(block_f[:], 0.0)
            for b in range(NBK - 1):
                dve.drain()
                V.scalar_tensor_tensor(block_f[:], step_no[:], steps_end[:, b:b + 1], block_f[:],
                                       ALU.is_ge, ALU.add)
            dve.drain()
            V.tensor_copy(block_i[:], block_f[:])
            dve.drain()
            dve.sem_inc(s_first, 1)

            def chunk_rows(chunk, c, last=False):
                t = bass.ds(chunk * CH, CH)
                for n, (a, z) in enumerate(PARTS):
                    dve.wait_ge(s_keyrow, chunk * len(PARTS) + (n + 1))
                    for k in range(a, z):
                        ins = V.scalar_tensor_tensor(same[:, k, :], bank[2 + n % 2][:, (k - a) * P:(k - a + 1) * P],
                                                     key_c[c][:, k:k + 1], after[:], ALU.is_equal, ALU.mult,
                                                     accum_out=rank[:, k:k + 1])
                    ins.then_inc(s_ranked, 1)
                V.tensor_copy(chunkA[c][:, :, C_NORM], norm_u[:, t])
                V.tensor_copy(chunkA[c][:, :, C_LOCAL], local_of[:, t])
                V.tensor_copy(chunkA[c][:, :, C_SRC], keyf[1][:, t])
                V.tensor_copy(chunkA[c][:, :, C_REL], rel_u[:, t])
                if not last:
                    chunk_hots(chunk + 1, 1 - c)
                dve.wait_ge(s_found, chunk + 1)
                V.tensor_tensor(slot_p[:], bank[4 + 2 * c][:, 0:CH * NBK].rearrange("p (t b) -> p t b", b=NBK),
                                in_blk[c][:], ALU.mult)
                dve.drain()
                V.tensor_reduce(slot_f[:], slot_p[:], AX_X, ALU.add)
                dve.drain()
                V.tensor_tensor(slot_f[:], slot_f[:], rank[:], ALU.add)
                dve.drain()
                V.tensor_copy(chunk_at[c][:], slot_f[:])
                dve.drain()
                dve.sem_inc(s_chunk, 1)

            dve.sem_inc(s_ranked, 2)
            dve.wait_ge(s_hist, NCH)
            chunk_hots(0, 0)
            for c in range(2):
                chunk_rows(c, c)
            with dve.Fori(1, NCH // 2 - 1) as i:
                for c in range(2):
                    dve.wait_ge(s_scat[c], i * (16 * CH))
                    chunk_rows(i * 2 + c, c)
            for c in range(2):
                dve.wait_ge(s_scat[c], (NCH // 2 - 1) * 16 * CH)
                chunk_rows(NCH - 2 + c, c, last=(c == 1))

            def root(values, ready):
                values().then_inc(s_sqin, 1)
                dve.wait_ge(s_sqout, ready)

            def layer_norm(ready):
                dve.drain()
                V.tensor_reduce(nstat[0][:], x[:], AX_X, ALU.add)
                dve.drain()
                V.tensor_scalar(nstat[2][:], nstat[0][:], 1.0 / FEAT, None, ALU.mult)
                dve.drain()
                V.tensor_tensor(h[:], x[:], wide(nstat[2][:], FEAT), ALU.subtract)
                dve.drain()
                V.tensor_tensor(tmp[:], h[:], h[:], ALU.mult)
                dve.drain()
                V.tensor_reduce(nstat[2][:], tmp[:], AX_X, ALU.add)
                dve.drain()
                root(lambda: V.tensor_scalar(nstat[0][:], nstat[2][:], 1.0 / FEAT, LN_EPS, ALU.mult, ALU.add), ready)
                V.reciprocal(nstat[2][:], nstat[1][:])
                dve.drain()
                V.tensor_tensor(h[:], h[:], wide(nstat[2][:], FEAT), ALU.mult)
                dve.drain()
                V.tensor_scalar(h[:], h[:], 0.0, None, ALU.max)
                dve.drain()

            def one_hots(step, p):
                for q in range(Q):
                    ins = V.tensor_scalar(hot[p][:, q, :], iota_row[:], row_loc[:, bass.ds(step * Q + q, 1)],
                                          None, ALU.is_equal)
                return ins

            def block_at(step):
                return dve.value_load(block_i[0:1, bass.ds(step, 1)], min_val=0, max_val=NBK - 1)

            def dense_turn(turn, ps):
                c0, c1 = TURN[turn]
                with dve.Fori(0, NB) as b:
                    first = of_block(dve, first_i, b, 0)
                    end = of_block(dve, end_i, b, 1)
                    with dve.Fori(first, end) as step:
                        for q in range(Q):
                            row_node = row_loc[:, bass.ds(step * Q + q, 1)]
                            dve.wait_ge(s_dsum[turn], step * SLOTS + (q * K + K))
                            V.tensor_scalar(hotb[:, q, :], iota_row[:], row_node, None, ALU.is_equal
                                            ).then_inc(s_hotb[turn], 1)
                            for j in range(q * K, (q + 1) * K):
                                dve.wait_ge(s_dsum[turn], step * SLOTS + (j + 1 + SLOTS - NSRC))
                                V.tensor_scalar(in_src[j % NSRC][:, 0:c1 - c0], node_no[:, c0:c1],
                                                edgeA[:, bass.ds(step * SLOTS + j, 1), C_SRC],
                                                None, ALU.is_equal).then_inc(s_src[turn], 1)
                            dve.wait_ge(ps.summed, step * Q + (q + 1))
                            ins = V.tensor_scalar(hot[0][:, q, :], iota_row[:], row_node, None, ALU.is_equal)
                            if turn == 0:
                                ins.then_inc(ps.hot, 1)
                            else:
                                dve.wait_ge(ps.landed[q], step * (16 * K) + 16 * K)
                                w = edgeA[:, bass.ds(step * SLOTS + q * K, K), C_NORM]
                                r = rows[0][:, q * K:(q + 1) * K, 0:FEAT]
                                V.tensor_tensor(r, r, w.unsqueeze(2).broadcast_to([P, K, FEAT]), ALU.mult)
                                dve.drain()
                                dve.sem_inc(ps.hot, 1)
                    for n, (lo, hi) in enumerate(BANKS[turn]):
                        dve.wait_ge(s_hi[turn], b * len(BANKS[turn]) + (n + 1))
                        V.tensor_tensor(hilo[:, 1, lo:hi], bank[n][:, 0:hi - lo], hilo[:, 0, lo:hi],
                                        ALU.subtract).then_inc(s_lo[turn], 1)
                    dve.wait_ge(ps.summed, end * Q + Q)
                    xb = x[:, bass.ds(b, 1), :].rearrange("p a c -> p (a c)")
                    if turn == 0:
                        ins = V.tensor_tensor(xb, xb, bank[7][:, 0:FEAT], ALU.add)
                    else:
                        ins = V.scalar_tensor_tensor(xb, bank[7][:, 0:FEAT], 0.0, xb, ALU.max, ALU.add)
                    ins.then_inc(ps.added, 1)
                dve.drain()

            for turn, ps in enumerate((pass0, pass1)):
                dve.sem_inc(ps.added, 1)
                dve.sem_inc(ps.summed, Q)
                dve.sem_inc(s_dsum[turn], SLOTS)
                dve.sem_inc(s_lo[turn], len(BANKS[turn]))
            for credit in (g_val, g_valA, pass3.summed):
                dve.sem_inc(credit, 1)
            dve.sem_inc(s_hT, 2)
            dve.sem_inc(s_fread, 2)
            pairsA, parts = pairs_of(dve), parts_of(dve)

            layer_norm(1)
            V.tensor_copy(tbl[:, :, 0:FEAT], h[:])
            dve.drain()
            dve.sem_inc(s_t0, 1)
            dve.wait_ge(s_edge, 16)
            V.tensor_copy(row_loc[:], edgeA[:].rearrange("p (g k) w -> p g k w", k=K)[:, :, 0, C_LOCAL])
            V.tensor_scalar(empty[:], edgeA[:, :, C_LOCAL], 0.0, FAR, ALU.is_lt, ALU.mult)
            dve.wait_ge(s_node_no, 1)
            dve.drain()
            dve.sem_inc(s_node_no, 1)
            dense_turn(0, pass0)
            root(lambda: V.tensor_scalar(nstat[0][:], counts[:], 1.0, None, ALU.add), 2)
            V.reciprocal(dinv[:], nstat[1][:])

            layer_norm(3)
            with dve.Fori(0, NBK // 2) as i:
                for p in range(2):
                    dve.wait_ge(s_hT, i * 2 + (p + 1))
                    V.tensor_copy(h_blk[p][:], h[:, bass.ds(i * 2 + p, 1), :].rearrange("p a c -> p (a c)")
                                  ).then_inc(s_hblk, 1)
            for p in range(2):
                dve.wait_ge(s_tab1[p], 16 * (NBK // 2))
            dve.wait_ge(s_node_no, 3)
            dense_turn(1, pass1)

            layer_norm(4)
            V.tensor_copy(hh, h[:])
            with dve.Fori(0, STEPS_L2) as k:
                dve.drain()
                V.tensor_tensor(tmp[:], h[:], wide(dinv[:], FEAT), ALU.mult)
                dve.drain()
                for part in range(3):
                    zp = zpart[:, :, part * FEAT:(part + 1) * FEAT]
                    left = tmp[:] if part == 0 else z_rest
                    V.tensor_copy(zp, left)
                    dve.drain()
                    if part < 2:
                        V.tensor_tensor(z_rest, left, zp, ALU.subtract)
                        dve.drain()
                dve.sem_inc(s_z, 1)
                dve.wait_ge(s_dused, (k + 1) * parts * NB + 2)
                for n in range(-(-NB // PER_BANK)):
                    lo, hi = n * PER_BANK, min((n + 1) * PER_BANK, NB)
                    V.tensor_tensor(tmp[:, lo:hi, :], tmp[:, lo:hi, :],
                                    bank[n][:, 0:(hi - lo) * FEAT].rearrange("p (b c) -> p b c", c=FEAT), ALU.add)
                dve.drain()
                V.tensor_tensor(tmp[:], tmp[:], wide(dinv[:], FEAT), ALU.mult)
                dve.drain()
                V.tensor_tensor(tmp[:], h[:], tmp[:], ALU.subtract)
                dve.drain()
                V.scalar_tensor_tensor(tmp[:], tmp[:], -GAMMA * 2.0 * (1.0 - LAMBDA_AMP), h[:], ALU.mult, ALU.add)
                dve.drain()
                V.tensor_tensor(tmp[:], tmp[:], hh, ALU.subtract)
                dve.drain()
                V.tensor_tensor(h[:], tmp[:], tmp[:], ALU.mult)
                dve.drain()
                V.tensor_reduce(nstat[2][:], h[:], AX_X, ALU.add)
                dve.drain()
                root(lambda: V.tensor_copy(nstat[0][:], nstat[2][:]), k + 5)
                V.tensor_scalar(nstat[2][:], nstat[1][:], 1e-30, None, ALU.max)
                V.tensor_scalar(nstat[0][:], nstat[1][:], GAMMA * LAMBDA_AMP, 0.0, ALU.subtract, ALU.max)
                dve.drain()
                V.reciprocal(nstat[2][:], nstat[2][:])
                dve.drain()
                V.tensor_tensor(nstat[0][:], nstat[0][:], nstat[2][:], ALU.mult)
                dve.drain()
                V.tensor_tensor(tmp[:], tmp[:], wide(nstat[0][:], FEAT), ALU.mult)
                dve.drain()
                V.tensor_tensor(h[:], hh, tmp[:], ALU.add)
            dve.drain()
            V.tensor_tensor(x[:], x[:], h[:], ALU.add)

            layer_norm(5 + STEPS_L2)
            dve.sem_inc(s_lwfree, 1)
            with dve.Fori(0, LAYERS) as l:
                V.tensor_scalar(h[:], h[:], 0.0, None, ALU.max)
                dve.wait_ge(s_lw, l * 64 + 64)
                V.tensor_copy(att_b[:], wide(att[:], P)).then_inc(s_attb, 1)
                dve.wait_ge(s_vec, l + 1)
                V.tensor_copy(vec[:].rearrange("p c k -> p (c k)"), bank[7][:, 0:2 * HEADS * AW])
                dve.drain()
                V.tensor_copy(tbl[:, :, 0:FEAT], h[:])
                tgt_v = a_tgt[:].rearrange("p (b h) -> p b h", h=HEADS)
                tmp_v = a_tmp[:].rearrange("p (b h) -> p b h", h=HEADS)
                for c in range(2 * HEADS):
                    w = vec[:, c:c + 1, 0:FEAT].broadcast_to([P, NBK, FEAT])
                    V.tensor_tensor(tmp[:], h[:], w, ALU.mult)
                    dve.drain()
                    dest = tbl[:, :, FEAT + c] if c < HEADS else tgt_v[:, :, c - HEADS]
                    V.tensor_reduce(dest, tmp[:], AX_X, ALU.add)
                    dve.drain()
                    if c == HEADS - 1:
                        dve.sem_inc(s_t3, 1)
                V.tensor_tensor(tmp_v, tgt_v, tbl[:, :, FEAT:FEAT + HEADS], ALU.add)
                dve.drain()
                V.tensor_tensor(tmp_v, tmp_v, vec[:, 0:HEADS, AW - 1].unsqueeze(1).broadcast_to([P, NBK, HEADS]), ALU.add)
                V.memset(acc[:], 0.0)
                dve.drain()
                V.scalar_tensor_tensor(a_max[:], a_tmp[:], 0.2, a_tmp[:], ALU.mult, ALU.max)
                av = acc[:].rearrange("p (b h c) -> p b h c", h=HEADS, c=AW)
                for hd in range(HEADS):
                    V.tensor_copy(av[:, :, hd, 0:FEAT], h[:])
                V.memset(accv[:, :, AW - 1], 1.0)
                dve.drain()

                def by_row(a):
                    return a.rearrange("p (q h) -> p q h", h=HEADS).unsqueeze(2).broadcast_to([P, Q, K, HEADS])

                def slots(a):
                    return a.rearrange("p (q k h) -> p q k h", k=K, h=HEADS)

                def attributes(step):
                    return edgeA[:, bass.ds(step * SLOTS, SLOTS), 0:EDGE_F + 1].unsqueeze(2).broadcast_to(
                        [P, SLOTS, HEADS, EDGE_F + 1])

                def targets(step, p):
                    blk = block_at(step)
                    V.tensor_copy(tgt_q[:], a_tgt[:, bass.ds(blk * HEADS, HEADS)])
                    one_hots(step, p)
                    dve.drain()
                    dve.sem_inc(pass3.hot, 1)
                    return blk

                def edge_part(step):
                    for q in range(Q):
                        V.tensor_scalar(far[:, q, :], iota_row[:], row_loc[:, bass.ds(step * Q + q, 1)],
                                        FAR, ALU.not_equal, ALU.mult)
                    av_e = vec[:, 0:HEADS, FEAT:AW].unsqueeze(1).broadcast_to([P, SLOTS, HEADS, EDGE_F + 1])
                    V.tensor_tensor(edge_p, attributes(step), av_e, ALU.mult)
                    dve.drain()
                    es = edge_s[:].rearrange("p (t h) -> p t h", h=HEADS)
                    V.tensor_reduce(es, edge_p, AX_X, ALU.add)
                    dve.drain()
                    V.tensor_tensor(es, es, wide(empty[:, bass.ds(step * SLOTS, SLOTS)], HEADS), ALU.add)
                    dve.drain()

                def score(number, p, turn):
                    es = edge_s[:].rearrange("p (t h) -> p t h", h=HEADS)
                    dve.wait_ge(pass3.landed[p], turn * (16 * SLOTS))
                    V.tensor_tensor(es, es, rows[p][:, :, FEAT:FEAT + HEADS], ALU.add)
                    dve.drain()
                    dve.wait_ge(g_tgte, number + 1)
                    V.tensor_tensor(slots(edge_s[:]), slots(edge_s[:]), by_row(bank[4][:, 0:Q * HEADS]), ALU.add)
                    dve.drain()
                    V.scalar_tensor_tensor(alpha[:], edge_s[:], 0.2, edge_s[:], ALU.mult, ALU.max)
                    dve.drain()
                    V.tensor_reduce(row_max[:].rearrange("p (q h) -> p q h", h=HEADS),
                                    alpha[:].rearrange("p (q k h) -> p q h k", k=K, h=HEADS), AX_X, ALU.max)
                    dve.drain()
                    for hd in range(HEADS):
                        for q in range(Q):
                            ins = V.scalar_tensor_tensor(scored[:, hd, q, :], hot[p][:, q, :],
                                                         row_max[:, q * 2 + hd:q * 2 + hd + 1], far[:, q, :],
                                                         ALU.mult, ALU.add)
                        ins.then_inc(g_scored, 1)

                def raise_max(blk, number, p):
                    for hd in range(HEADS):
                        dve.wait_ge(g_across, number * HEADS + (hd + 1))
                        V.tensor_reduce(gmax[:, hd:hd + 1], bank[2 + hd][:, 0:Q * P], AX_X, ALU.max)
                    dve.drain()
                    mx = a_max[:, bass.ds(blk * HEADS, HEADS)]
                    V.tensor_tensor(newmax[:], mx, gmax[:], ALU.max)
                    dve.drain()
                    V.tensor_tensor(drop[p][:], mx, newmax[:], ALU.subtract)
                    dve.drain()
                    dve.sem_inc(g_newmax, 1)
                    V.tensor_copy(mx, newmax[:])

                def below_max(number):
                    dve.wait_ge(g_maxe, number + 1)
                    V.tensor_tensor(slots(argx[:]), slots(alpha[:]), by_row(bank[5][:, 0:Q * HEADS]),
                                    ALU.subtract).then_inc(g_arg, 1)

                def weigh(step, p):
                    exv = ex[:].rearrange("p (t h) -> p t h", h=HEADS)
                    V.tensor_tensor(val[:, :, 0, 0:FEAT], rows[p][:, :, 0:FEAT], wide(exv[:, :, 0], FEAT), ALU.mult)
                    V.tensor_tensor(val[:, ACT_SLOTS:, 1, 0:FEAT], rows[p][:, ACT_SLOTS:, 0:FEAT],
                                    wide(exv[:, ACT_SLOTS:, 1], FEAT), ALU.mult)
                    V.tensor_tensor(val[:, :, :, FEAT:AW], attributes(step),
                                    exv.unsqueeze(3).broadcast_to([P, SLOTS, HEADS, EDGE_F + 1]), ALU.mult)
                    dve.drain()
                    dve.sem_inc(g_val, 1)

                def add(blk, n, ahead, p):
                    dve.wait_ge(g_keep, ahead)
                    dve.wait_ge(pass3.summed, n + 2)
                    for hd in range(HEADS):
                        a = acc[:, bass.ds(blk * (HEADS * AW) + hd * AW, AW)]
                        V.scalar_tensor_tensor(a, a, keep[p][:, hd:hd + 1], bank[6 + p][:, hd * AW:(hd + 1) * AW],
                                               ALU.mult, ALU.add)
                    dve.drain()

                first = l * (pairsA * 2 + 1)
                blk = targets(0, 0)
                edge_part(0)
                score(first, 0, l * (pairsA + 1) + 1)
                raise_max(blk, first, 0)
                below_max(first)
                with dve.Fori(0, pairsA) as i:
                    blk = None
                    for p in range(2):
                        step = i * 2 + p
                        n = l * pairsA * 2 + i * 2 + p
                        ahead = first + i * 2 + (p + 1)
                        turn = l * pairsA + i + 1 if p == 0 else l * (pairsA + 1) + i + 2
                        before_blk = blk
                        blk = targets(step + 1, 1 - p)
                        dve.wait_ge(g_ex, ahead)
                        weigh(step, p)
                        edge_part(step + 1)
                        score(ahead, 1 - p, turn)
                        add(block_at(step) if p == 0 else before_blk, n, ahead, p)
                        raise_max(blk, ahead, 1 - p)
                        below_max(ahead)
                dve.drain()

                V.tensor_scalar(a_tmp[:], accv[:, :, AW - 1], 1e-16, None, ALU.add)
                dve.drain()
                V.reciprocal(a_tmp[:], a_tmp[:])
                dve.drain()
                V.tensor_scalar(a_tmp[:], a_tmp[:], 1.0 / HEADS, None, ALU.mult)
                dve.drain()

                def mean_part(m, b, p, first=False):
                    if not first:
                        dve.wait_ge(s_fT, m - 1)
                    c = FB * HEADS
                    V.tensor_tensor(agg[p], acc[:, bass.ds(b * (c * AW), c * AW)].rearrange("p (c k) -> p c k", k=AW),
                                    wide(a_tmp[:, bass.ds(b * c, c)], AW), ALU.mult).then_inc(s_fb, 1)

                def biased(m, b, p):
                    dve.wait_ge(s_fo, m + 1)
                    V.tensor_tensor(h[:, bass.ds(b * FB, FB), :], bank[2 + p][:, 0:FB * FEAT].rearrange("p (b c) -> p b c", c=FEAT),
                                    bias[:].unsqueeze(1).broadcast_to([P, FB, FEAT]), ALU.add).then_inc(s_fread, 1)

                for p in range(2):
                    mean_part(l * NF + p, p, p, first=True)
                with dve.Fori(0, NF // 2 - 1) as b:
                    for p in range(2):
                        mean_part(l * NF + b * 2 + (p + 2), b * 2 + (p + 2), p)
                        biased(l * NF + b * 2 + p, b * 2 + p, p)
                mean_part(l * NF + NF - 1, NF - 1, 0)
                for b in range(NF - 3, NF):
                    biased(l * NF + b, b, b % 2)
                dve.drain()
                dve.sem_inc(s_lwfree, 1)
            dve.drain()
            V.tensor_tensor(x[:], x[:], h[:], ALU.add).then_inc(s_done, 1)


def kernel(x, src, dst, edge_attr_16, edge_type_16, edge_weight1, L1_gnn_weight, L3_gnn_weights,
           L3_gnn_biases, L3_gnn_edge_ws, L3_gnn_edge_bs, L3_gnn_atts):
    import numpy as np
    import concourse.bacc as bacc
    from concourse.bass_utils import run_bass_kernel_spmd

    nodes, edges = x.shape[0], src.shape[0]
    tiles, blocks, _ = sizes(nodes, edges)
    pad = tiles * P - edges

    def by_tile(a, fill):
        a = np.asarray(a)
        a = np.concatenate([a, np.full((pad,) + a.shape[1:], fill, a.dtype)])
        return np.ascontiguousarray(a.reshape((tiles, P) + a.shape[1:]).swapaxes(0, 1).reshape(P, -1))

    xp = np.concatenate([np.asarray(x), np.zeros((blocks * P - nodes, FEAT), np.float32)])
    xp = np.ascontiguousarray(xp.reshape(blocks, P, FEAT).swapaxes(0, 1).reshape(P, -1))
    w = np.asarray(L3_gnn_weights)
    layers = w.shape[0]
    w = w.reshape(layers, FEAT, HEADS, FEAT).transpose(0, 2, 1, 3)
    ew = np.asarray(L3_gnn_edge_ws).reshape(layers, HEADS, FEAT, EDGE_F).transpose(0, 1, 3, 2)
    eb = np.asarray(L3_gnn_edge_bs).reshape(layers, HEADS, 1, FEAT)
    wcat = np.concatenate([w, ew, eb], axis=2)
    atts = np.asarray(L3_gnn_atts).reshape(layers, HEADS, 2, FEAT)
    pad_key = (nodes // P + 1) * P - 1
    arrays = {
        "x_in": xp,
        "src_in": by_tile(src, pad_key),
        "dst_in": by_tile(dst, pad_key),
        "type_in": by_tile(edge_type_16, 0),
        "norm_in": by_tile(edge_weight1, 0),
        "attr_in": by_tile(edge_attr_16, 0),
        "w1_in": np.ascontiguousarray(np.asarray(L1_gnn_weight).transpose(1, 0, 2).reshape(FEAT, -1)),
        "wcat_in": np.ascontiguousarray(wcat.transpose(0, 2, 1, 3).reshape(layers, AW, -1)),
        "wcatT_in": np.ascontiguousarray(wcat.transpose(0, 3, 1, 2).reshape(layers, FEAT, -1)),
        "att_in": np.ascontiguousarray(atts[:, :, ::-1].transpose(0, 3, 2, 1).reshape(layers, FEAT, -1)),
        "bias_in": np.ascontiguousarray(np.broadcast_to(np.asarray(L3_gnn_biases)[:, None], (layers, P, FEAT)).reshape(-1, FEAT)),
    }
    nc = bacc.Bacc("TRN2", target_bir_lowering=False, num_devices=1)
    args = {n: nc.dram_tensor(n, a.shape, mybir.dt.from_np(a.dtype), kind="ExternalInput").ap()
            for n, a in arrays.items()}
    out = nc.dram_tensor("out", (P, blocks * FEAT), F32, kind="ExternalOutput").ap()
    gnn_kernel(nc, nodes, out=out, **args)
    r = run_bass_kernel_spmd(nc, [arrays], core_ids=[0])
    got = r.results[0]["out"].reshape(P, blocks, FEAT).swapaxes(0, 1).reshape(-1, FEAT)[:nodes]
    return np.ascontiguousarray(got)
```
